# Optimizing a Trainium2 kernel written in Bass

```python
import numpy as np
import jax
import jax.numpy as jnp

def _softmax(x, axis=-1):
    return jax.nn.softmax(x, axis=axis)

def _gelu(x):
    return jax.nn.gelu(x, approximate=True)

def _silu(x):
    return jax.nn.silu(x)

def _sigmoid(x):
    return jax.nn.sigmoid(x)

def _layernorm(x, axis=-1, eps=1e-05):
    m = jnp.mean(x, axis=axis, keepdims=True)
    v = jnp.var(x, axis=axis, keepdims=True)
    return (x - m) / jnp.sqrt(v + eps)

def _scatter_add(tgt, idx, src, axis=0):
    return tgt.at[idx].add(src)

def _segment_sum(src, seg, n):
    return jax.ops.segment_sum(src, seg, n)
kernel_name = 'mk_adaln_d1_jaxref_r2_58bae6'

def setup_inputs(seed: int=0):
    np.random.seed(seed)
    _w = jnp.asarray

    def _L0_attn_setup():
        import jax, jax.numpy as jnp
        import numpy as np
        B, T, D, H = (4, 512, 512, 16)
        key = jax.random.key(seed)
        ks = jax.random.split(key, 7)
        x = jax.random.normal(ks[0], (B, T, D), dtype=jnp.float32)
        scale = 0.02
        Wq = jax.random.normal(ks[1], (D, D), dtype=jnp.float32) * scale
        Wk = jax.random.normal(ks[2], (D, D), dtype=jnp.float32) * scale
        Wv = jax.random.normal(ks[3], (D, D), dtype=jnp.float32) * scale
        bq = jax.random.normal(ks[4], (D,), dtype=jnp.float32) * scale
        bk = jax.random.normal(ks[5], (D,), dtype=jnp.float32) * scale
        bv = jax.random.normal(ks[6], (D,), dtype=jnp.float32) * scale
        temperature = jnp.ones((H, 1, 1), dtype=jnp.float32)
        return {'x': x, 'Wq': Wq, 'bq': bq, 'Wk': Wk, 'bk': bk, 'Wv': Wv, 'bv': bv, 'temperature': temperature}
    _L0_attn_in = _L0_attn_setup()

    def _L0_ffn_setup():
        import jax, jax.numpy as jnp
        import numpy as np
        CAPACITY_FACTOR = 0.5
        key = jax.random.key(seed)
        ks = jax.random.split(key, 5)
        B, S, D, F = (4, 2048, 512, 2048)
        scale_in = 1.0 / np.sqrt(D)
        scale_ff = 1.0 / np.sqrt(F)
        return {'hidden_states': jax.random.normal(ks[0], (B, S, D), dtype=jnp.float32), 'w_router': jax.random.normal(ks[1], (D,), dtype=jnp.float32) * scale_in, 'W1': jax.random.normal(ks[2], (D, F), dtype=jnp.float32) * scale_in, 'b1': jnp.zeros((F,), dtype=jnp.float32), 'W2': jax.random.normal(ks[3], (F, D), dtype=jnp.float32) * scale_ff, 'b2': jnp.zeros((D,), dtype=jnp.float32)}
    _L0_ffn_in = _L0_ffn_setup()
    _L0_c = _w((lambda *s: np.random.randn(*s).astype(np.float32) * 0.05)(8, 512))
    _L0_wmod = _w((lambda *s: np.random.randn(*s).astype(np.float32) * 0.05)(512, 6 * 512) * 512 ** (-0.5))
    _d = {'L0_attn_x': _L0_attn_in['x'], 'L0_attn_Wq': _L0_attn_in['Wq'], 'L0_attn_bq': _L0_attn_in['bq'], 'L0_attn_Wk': _L0_attn_in['Wk'], 'L0_attn_bk': _L0_attn_in['bk'], 'L0_attn_Wv': _L0_attn_in['Wv'], 'L0_attn_bv': _L0_attn_in['bv'], 'L0_attn_temperature': _L0_attn_in['temperature'], 'L0_ffn_w_router': _L0_ffn_in['w_router'], 'L0_ffn_W1': _L0_ffn_in['W1'], 'L0_ffn_b1': _L0_ffn_in['b1'], 'L0_ffn_W2': _L0_ffn_in['W2'], 'L0_ffn_b2': _L0_ffn_in['b2'], 'L0_c': _L0_c, 'L0_wmod': _L0_wmod}
    _x0 = _d['L0_attn_x']
    _d['L0_attn_x'] = jax.random.normal(jax.random.fold_in(jax.random.key(seed), 1), (8, 1024, 512), dtype=_x0.dtype)
    del _x0
    return _d

def reference(L0_attn_x, L0_attn_Wq, L0_attn_bq, L0_attn_Wk, L0_attn_bk, L0_attn_Wv, L0_attn_bv, L0_attn_temperature, L0_ffn_w_router, L0_ffn_W1, L0_ffn_b1, L0_ffn_W2, L0_ffn_b2, L0_c, L0_wmod):

    def _L0_attn_ref(x, Wq, bq, Wk, bk, Wv, bv, temperature):
        import jax, jax.numpy as jnp
        import numpy as np
        B, T, D, H = (4, 512, 512, 16)
        b, t, d = x.shape
        h = temperature.shape[0]
        dh = d // h
        q = (x @ Wq + bq).reshape(b, h, dh, t)
        k = (x @ Wk + bk).reshape(b, h, dh, t)
        v = (x @ Wv + bv).reshape(b, h, dh, t)
        attn = jnp.einsum('bhdt,bhds->bhts', k, v) * temperature
        attn = jax.nn.softmax(attn, axis=-1)
        out = jnp.einsum('bhdt,bhts->bhds', q, attn)
        return out.reshape(b, t, d)

    def _L0_ffn_ref(hidden_states, w_router, W1, b1, W2, b2):
        import jax, jax.numpy as jnp
        import numpy as np
        CAPACITY_FACTOR = 0.5
        'Mixture-of-Depths block: route top-k tokens through an FFN inner block,\n            scatter back with sigmoid router weights; bypassed tokens pass through.'
        B, S, D = hidden_states.shape
        k = int(S * CAPACITY_FACTOR)
        scores = jnp.einsum('bsd,d->bs', hidden_states, w_router)
        top_scores, top_idx = jax.lax.top_k(scores, k)
        weights = jax.nn.sigmoid(top_scores)
        selected = jnp.take_along_axis(hidden_states, top_idx[:, :, None], axis=1)
        h = jax.nn.gelu(jnp.einsum('bkd,df->bkf', selected, W1) + b1)
        processed = jnp.einsum('bkf,fd->bkd', h, W2) + b2
        update = weights[:, :, None] * processed

        def scatter_one(xb, ib, ub):
            return xb.at[ib].add(ub)
        output = jax.vmap(scatter_one)(hidden_states, top_idx, update)
        return output
    x = L0_attn_x
    mod = (_silu(L0_c) @ L0_wmod).reshape(L0_c.shape[0], 6, 1, -1)
    sa, ca, ga, sb, cb, gb = (mod[:, 0], mod[:, 1], mod[:, 2], mod[:, 3], mod[:, 4], mod[:, 5])
    ga = (2 * (ga >= 0) - 1) * jnp.maximum(jnp.abs(ga), 0.25)
    gb = (2 * (gb >= 0) - 1) * jnp.maximum(jnp.abs(gb), 0.25)
    h = _layernorm(x, axis=-1) * (1 + ca) + sa
    x = x + ga * _L0_attn_ref(h, L0_attn_Wq, L0_attn_bq, L0_attn_Wk, L0_attn_bk, L0_attn_Wv, L0_attn_bv, L0_attn_temperature)
    h = _layernorm(x, axis=-1) * (1 + cb) + sb
    x = x + gb * _L0_ffn_ref(h, L0_ffn_w_router, L0_ffn_W1, L0_ffn_b1, L0_ffn_W2, L0_ffn_b2)
    return x

_drawn_inputs = setup_inputs


def setup_inputs(seed=0):
    import zlib

    import numpy as np

    out = dict(_drawn_inputs(seed))
    spreads = {'L0_attn_temperature': (1.0, 0.6), 'L0_ffn_b1': (0.0, 0.8), 'L0_ffn_b2': (0.0, 0.711)}
    factors = {'L0_attn_Wq': 6.634,
     'L0_attn_bq': 8.0,
     'L0_attn_Wk': 7.442,
     'L0_attn_bk': 8.0,
     'L0_attn_Wv': 7.631,
     'L0_attn_bv': 8.0}
    for name, (base, spread) in spreads.items():
        noise = np.random.default_rng([zlib.crc32(name.encode()), seed]).standard_normal(out[name].shape)
        drawn = base * np.exp(spread * noise) if base else spread * noise
        out[name] = jnp.asarray(drawn.astype(out[name].dtype))
    for name, factor in factors.items():
        out[name] = (out[name] * factor).astype(out[name].dtype)
    return out
```

```python
from contextlib import ExitStack

import concourse.bass as bass
from concourse import mybir

P = 128
B, T, D = 8, 1024, 512
H = 16
DH = D // H
F = 2048
KEEP = T // 2
CC = D // P
FC = F // P
HG = P // DH
TG = HG * DH * 2
GB = T // TG
NG = B * GB
NQ = T // P
WS = 64.0
EPS = 1e-5
BIG = 1.0e6
GATE_MIN = 0.25

ALU = mybir.AluOpType
ACT = mybir.ActivationFunctionType
AX = mybir.AxisListType
F32 = mybir.dt.float32
F16 = mybir.dt.float16
BF16 = mybir.dt.bfloat16
I32 = mybir.dt.int32


def attention_phase(nc, x, w_qkv, b_qkv, temperature, w_router, c, w_mod, out, h_rows, mod_rows, scores):
    Wq, Wk, Wv = w_qkv
    bq, bk, bv = b_qkv
    x_g = x.rearrange("b (g q p) d -> (b g) q p d", g=GB, p=2)
    out_g = out.rearrange("b (g q p) d -> (b g) q p d", g=GB, p=2)
    h_g = h_rows.rearrange("(n q p) d -> n q p d", n=NG, p=2)

    with ExitStack() as ctx:
        def sb(name, shape, dt):
            return ctx.enter_context(nc.sbuf_tensor(name, shape, dt))

        def pb(name, shape):
            return ctx.enter_context(nc.psum_tensor(name, shape, F32))

        def sem(name):
            return ctx.enter_context(nc.semaphore(name))

        wq16 = sb("wq16", [P, 2, CC, D], F16)
        wk16 = sb("wk16", [P, 2, CC, D], F16)
        wv16 = sb("wv16", [P, 2, CC, D], F16)
        ident = sb("ident", [P, P], F32)
        bq_col = sb("bq_col", [P, CC], F32)
        bk_row = sb("bk_row", [P, D], F32)
        bv_row = sb("bv_row", [P, D], F32)
        bkt_row = sb("bkt_row", [P, GB, D], F32)
        router_row = sb("router_row", [P, D], F32)
        temp_col = sb("temp_col", [P, GB], F32)
        tempw_col = sb("tempw_col", [P, GB], F32)
        mod_table = sb("mod_table", [P, B + 1, 2 * CC], F32)
        mod_now = sb("mod_now", [P, 2 * CC], F32)
        rows = sb("rows", [P, 4, D], F32)
        minus_half = sb("minus_half", [P, 2], F32)
        warm = sb("warm", [P, 1], F32)
        xt = [sb(f"xt{i}", [P, 2, D], F32) for i in range(4)]
        xhat = sb("xhat", [P, 2, D], F32)
        stats1 = sb("stats1", [P, 2, 6], F32)
        mv1 = sb("mv1", [P, 2, 2], F32)
        var1 = sb("var1", [P, 2], F32)
        nmean1 = sb("nmean1", [P, 2], F32)
        rstd1 = sb("rstd1", [P, 2], F32)
        hT32 = sb("hT32", [P, CC, 2 * P], F32)
        hT16 = sb("hT16", [P, 2, CC, 2 * P], F16)
        kv32 = [sb(f"kv32_{i}", [P, D], F32) for i in range(2)]
        k16 = sb("k16", [P, 2, 2 * D], F16)
        v16 = sb("v16", [P, 2, 2 * D], F16)
        stacks = [sb(f"stacks{i}", [P, 2, HG, 2 * D], F16) for i in range(2)]
        qT = [sb(f"qT{i}", [P, CC, 2 * P], F32) for i in range(2)]
        qn = sb("qn", [P, 2, HG, DH], F32)
        probs = sb("probs", [P, 2, HG, T], F32)
        nmax = sb("nmax", [P, 2, HG], F32)
        rsum = sb("rsum", [P, 2, HG], F32)
        rinv = sb("rinv", [P, 2, HG], F32)
        x2 = sb("x2", [P, 2, D], F32)
        stats2 = sb("stats2", [P, 2, 6], F32)
        mv2 = sb("mv2", [P, 2, 2], F32)
        var2 = sb("var2", [P, 2], F32)
        nmean2 = sb("nmean2", [P, 2], F32)
        rstd2 = sb("rstd2", [P, 2], F32)
        xhat2 = sb("xhat2", [P, 2, D], F32)
        hbuf = sb("hbuf", [P, 2, 2, D], F32)
        base = sb("base", [P, 2, 2, D], F32)
        dot_out = sb("dot_out", [P, 2, D], F32)
        c_sb = sb("c_sb", [B, D], F32)
        c_e = sb("c_e", [B, D], F32)
        cT = sb("cT", [P, CC, B], F32)
        mod_b = sb("mod_b", [B, 4, D], F32)
        mod_t = sb("mod_t", [B, 2, D], F32)
        sign, size = xhat2[0:B, 0, :], xhat2[0:B, 1, :]

        acc = pb("acc", [P, 2 * D])
        sc = [pb(f"sc{i}", [P, 2 * D]) for i in range(2)]
        pj = [pb(f"pj{i}", [P, D]) for i in range(2)]

        s_c = sem("s_c")
        s_in = sem("s_in")
        s_w = [sem(f"s_w{i}") for i in range(3)]
        s_wm = [sem(f"s_wm{i}") for i in range(6)]
        s_x = [sem(f"s_x{i}") for i in range(4)]
        s_rows = sem("s_rows")
        s_modst = sem("s_modst")
        s_stk = [[sem(f"s_stk{k}{i}") for i in range(2)] for k in range(2)]
        s_st = [sem(f"s_st{i}") for i in range(2)]
        s_id = sem("s_id")
        s_idle = sem("s_idle")
        s_const = sem("s_const")
        s_v = sem("s_v")
        s_wsplit = sem("s_wsplit")
        s_ce = sem("s_ce")
        s_silu = sem("s_silu")
        s_ct = sem("s_ct")
        s_ctc = sem("s_ctc")
        s_mod = sem("s_mod")
        s_modc = sem("s_modc")
        s_modv = sem("s_modv")
        s_mt = sem("s_mt")
        s_table = sem("s_table")
        s_now = sem("s_now")
        s_bn1 = sem("s_bn1")
        s_var1 = sem("s_var1")
        s_r1 = sem("s_r1")
        s_xhat = sem("s_xhat")
        t_pe = sem("t_pe")
        t_evac = sem("t_evac")
        s_hi = sem("s_hi")
        s_ht = sem("s_ht")
        kv_pe = sem("kv_pe")
        kv_evac = sem("kv_evac")
        kv_hi = sem("kv_hi")
        kv_split = sem("kv_split")
        q_pe = sem("q_pe")
        q_evac = sem("q_evac")
        score_pe = sem("score_pe")
        max_done = sem("max_done")
        exp_done = sem("exp_done")
        inv_done = sem("inv_done")
        qn_done = sem("qn_done")
        pv_done = sem("pv_done")
        acc_free = sem("acc_free")
        x2_done = sem("x2_done")
        s_bn2 = sem("s_bn2")
        s_agg1 = sem("s_agg1")
        s_agg2 = sem("s_agg2")
        s_dot = sem("s_dot")
        s_var2 = sem("s_var2")
        s_r2 = sem("s_r2")
        s_xh2 = sem("s_xh2")
        s_hm = sem("s_hm")
        post_done = sem("post_done")

        block = ctx.enter_context(nc.Block())

        wm_stage = [probs[:, j // 2, 2 * (j % 2):2 * (j % 2) + 2, :].rearrange("p a (b n) -> p (a b) n", n=D) for j in range(4)]
        wm_stage += [stacks[1][:, j].bitcast(F32).rearrange("p a n -> p (a n)").rearrange("p (c n) -> p c n", c=CC) for j in range(2)]
        w_stage = [stacks[0][:, j].bitcast(F32).rearrange("p a n -> p (a n)").rearrange("p (c n) -> p c n", c=CC) for j in range(2)]
        w_stage += [hbuf[:].rearrange("p a b n -> p (a b) n")]
        MOD_ORDER = (1, 0, 2, 3, 4, 5)

        def turn(n_static, b):
            return lambda per, off: b * (GB * per) + off

        @block.sync
        def _(sp):
            for i in range(2):
                sp.sem_inc(s_st[i], 16)
            sp.dma_start(c_sb[:], c).then_inc(s_c, 16)
            sp.dma_start(xt[0][:], x_g[0]).then_inc(s_x[0], 16)

            def stage_mod(j):
                m = MOD_ORDER[j]
                sp.dma_start(wm_stage[j], w_mod[:, m * D:(m + 1) * D].rearrange("(c p) n -> p c n", p=P)).then_inc(s_wm[j], 16)

            stage_mod(0)
            stage_mod(1)
            for k, w in enumerate((Wk, Wv, Wq)):
                sp.dma_start(w_stage[k], w.rearrange("(c p) n -> p c n", p=P)).then_inc(s_w[k], 16)
            sp.dma_start(bk_row[:], bk.partition_broadcast(P)).then_inc(s_in, 16)
            sp.dma_start(bv_row[:], bv.partition_broadcast(P)).then_inc(s_in, 16)
            sp.dma_start(router_row[:], w_router.partition_broadcast(P)).then_inc(s_in, 16)
            with nc.allow_non_contiguous_dma(reason="512 biases and 16 temperatures, once"):
                sp.dma_start(bq_col[:], bq.rearrange("(c p) -> p c", p=P)).then_inc(s_in, 16)
                t_hq = temperature.rearrange("(g q) a b -> q (g a b)", q=HG)
                for hq in range(HG):
                    sp.dma_start(temp_col[DH * hq:DH * (hq + 1), :], t_hq[hq].partition_broadcast(DH)).then_inc(s_in, 16)
            for i in (1, 2):
                sp.dma_start(xt[i][:], x_g[i]).then_inc(s_x[i], 16)
            for j in range(2, 6):
                stage_mod(j)

            def replicate(m_par, k, split_count):
                src, parts = ((k16, (0, 0, 1, 1)), (v16, (0, 1, 0, 1)))[k]
                sp.wait_ge(kv_split, split_count)
                for hq in range(HG):
                    for blk in range(P // DH):
                        sp.dma_start(stacks[m_par][DH * blk:DH * (blk + 1), k, hq, :],
                                     src[DH * hq:DH * (hq + 1), parts[blk], :]).then_inc(s_stk[k][m_par], 16)

            sp.wait_ge(s_wsplit, 6)
            replicate(0, 0, 2)
            replicate(0, 1, 4)
            sp.wait_ge(s_modv, 1)
            sp.dma_start(mod_rows, mod_b[:]).then_inc(s_modst, 16)
            sp.wait_ge(s_modst, 16)
            with sp.Fori(0, B) as b:
                ahead = [sp.snap(b * GB + g + 3 if g + 3 < GB else ((b + 1) % B) * GB + (g + 3) % GB) for g in range(GB)]
                for g in range(GB):
                    sp.wait_ge(x2_done, b * GB + g + 1)
                    sp.dma_start(xt[(g + 3) % 4][:], x_g[ahead[g]]).then_inc(s_x[(g + 3) % 4], 16)
                    if g == 0:
                        sp.wait_ge(post_done, b * GB + 1)
                        for j in range(4):
                            sp.dma_start(rows[:, j, :], mod_rows[b, j].partition_broadcast(P)).then_inc(s_rows, 16)
                    sp.wait_ge(pv_done, b * GB * NQ + g * NQ + 1)
                    sp.sem_inc(s_idle, 1)
                    replicate((g + 1) % 2, 0, b * GB * 4 + 4 * (g + 1) + 2)
                    replicate((g + 1) % 2, 1, b * GB * 4 + 4 * (g + 1) + 4)
                    sp.wait_ge(post_done, b * GB + g + 1 + 1)
                    sp.dma_start(h_g[b * GB + g], hbuf[:, g % 2]).then_inc(s_st[g % 2], 16)
                    sp.dma_start(out_g[b * GB + g], base[:, g % 2]).then_inc(s_st[g % 2], 16)
            for i in range(2):
                sp.wait_ge(s_st[i], 32 * NG // 2 + 16)
                for k in range(2):
                    sp.wait_ge(s_stk[k][i], 256 * (NG // 2 + 1 - i))
            for i in range(4):
                sp.wait_ge(s_x[i], 16 * (NG // 4 + (i < 3)))

        def stk_count(b, g_next):
            return b * (256 * GB // 2) + 256 * (g_next // 2 + 1)

        @block.tensor
        def _(pe):
            def scores_of(quad_g, i, hq, count):
                par = quad_g % 2
                u = hq % 2
                pe.wait_ge(exp_done, count)
                for half in range(2):
                    mm = nc.tensor.matmul(sc[u][:, half * D:(half + 1) * D],
                                          stacks[par][:, 0, hq, i * P:(i + 1) * P],
                                          stacks[par][:, 1, hq, half * D:(half + 1) * D], start=True, stop=True)
                mm.then_inc(score_pe, 1)

            def kv_slice(kk, free, count):
                w, p = (wk16, wv16)[kk // 2], kk % 2
                if free is not None:
                    pe.wait_ge(kv_evac, free)
                terms = [(cc, a, z) for cc in range(CC) for a, z in ((0, 0), (1, 0), (0, 1))]
                for t, (cc, a, z) in enumerate(terms):
                    mm = nc.tensor.matmul(pj[kk % 2][:], hT16[:, a, cc, p * P:(p + 1) * P], w[:, z, cc, :],
                                          start=(t == 0), stop=(t == len(terms) - 1))
                    if t == 5:
                        yield
                mm.then_inc(kv_pe, 1)

            def q_slice(s, free):
                pe.wait_ge(kv_evac, free)
                for ci in range(2):
                    co = 2 * s + ci
                    terms = [(cc, a, z) for cc in range(CC) for a, z in ((0, 0), (1, 0), (0, 1))]
                    for t, (cc, a, z) in enumerate(terms):
                        mm = nc.tensor.matmul(pj[s][:, ci * 2 * P:(ci + 1) * 2 * P],
                                              wq16[:, z, cc, co * P:(co + 1) * P], hT16[:, a, cc, :],
                                              start=(t == 0), stop=(t == len(terms) - 1))
                    if ci == 0:
                        yield
                mm.then_inc(q_pe, 1)

            def t_slice(s, xh, free):
                if xh is not None:
                    pe.wait_ge(s_xhat, xh)
                if free is not None:
                    pe.wait_ge(q_evac, free)
                for ci in range(2):
                    for p in range(2):
                        mm = nc.tensor.transpose(pj[s][:, ci * 2 * P + p * P:ci * 2 * P + (p + 1) * P],
                                                 xhat[:, p, (2 * s + ci) * P:(2 * s + ci + 1) * P], ident[:])
                mm.then_inc(t_pe, 1)
                return iter(())

            def pv_half(g, i, half, last_inc=False):
                for hq in range(HG):
                    mm = nc.tensor.matmul(acc[DH * hq:DH * (hq + 1), half * D:(half + 1) * D],
                                          qn[:, i % 2, hq, :], probs[:, i % 2, hq, half * D:(half + 1) * D],
                                          start=(i == 0), stop=(i == NQ - 1))
                if half == 1:
                    mm.then_inc(pv_done, 1)

            pe.sem_inc(pv_done, 1)
            pe.wait_ge(s_id, 2)
            pe.wait_ge(s_silu, 1)
            for cc in range(CC):
                mm = nc.tensor.transpose(pj[0][:, cc * B:(cc + 1) * B], c_e[:, cc * P:(cc + 1) * P], ident[0:B, 0:B])
            mm.then_inc(s_ct, 1)
            pe.wait_ge(s_ctc, 1)
            mod_banks = (sc[0][0:B, 0:D], sc[0][0:B, D:2 * D], sc[1][0:B, 0:D], sc[1][0:B, D:2 * D])

            def modulate(j):
                pe.wait_ge(s_wm[j], 16)
                for cc in range(CC):
                    mm = nc.tensor.matmul(mod_banks[j % 4], cT[:, cc, :], wm_stage[j][:, cc, :], start=(cc == 0), stop=(cc == CC - 1))
                mm.then_inc(s_mod, 1)

            modulate(0)
            modulate(1)
            pe.wait_ge(s_mt, 1)
            for k in range(2 * CC):
                src = mod_t[:, k // CC, (k % CC) * P:(k % CC + 1) * P]
                mm = nc.tensor.transpose(pj[1][:, k * B:(k + 1) * B], src, ident[0:B, 0:B])
            mm.then_inc(s_ct, 1)
            t_slice(0, 1, None)
            pe.wait_ge(s_table, 1)
            t_slice(1, None, None)
            pe.wait_ge(s_ht, 1)
            pe.wait_ge(s_wsplit, 6)
            for kk in range(4):
                for _ in kv_slice(kk, kk - 1 if kk >= 2 else None, 0):
                    pass
            for s in range(2):
                for _ in q_slice(s, 3 + s):
                    pass
            t_slice(0, 2, 1)
            t_slice(1, None, 2)
            for j in range(2, 6):
                modulate(j)
            for k in range(2):
                pe.wait_ge(s_stk[k][0], 256)
            pe.wait_ge(s_modc, 1)
            for hq in range(HG):
                scores_of(0, 0, hq, hq)

            with pe.Fori(0, B) as b:
                for g in range(GB):
                    m4 = b * GB * 4 + 4 * (g + 1)
                    m2 = b * GB * 2 + 2 * (g + 1)
                    for i in range(NQ):
                        if i == 0:
                            pe.wait_ge(s_ht, b * GB + g + 2)
                        if i < 4:
                            piece = kv_slice(i, m4 + i - 1 if i >= 2 else None, 0)
                        elif i < 6:
                            piece = q_slice(i - 4, m4 + 3 + i - 4)
                        else:
                            piece = None
                        qg, qi = (g, i + 1) if i + 1 < NQ else (g + 1, 0)
                        unit = b * (GB * NQ * HG) + (g * NQ + i + 1) * HG
                        if qi == 0:
                            for k in range(2):
                                pe.wait_ge(s_stk[k][qg % 2], stk_count(b, g + 1))
                        scores_of(qg, qi, 0, unit + 0)
                        if piece is not None:
                            next(piece, None)
                        scores_of(qg, qi, 1, unit + 1)
                        if piece is not None:
                            for _ in piece:
                                pass
                        else:
                            t_slice(i - 6, b * GB + g + 3, m2 + i - 5)
                        scores_of(qg, qi, 2, unit + 2)
                        pe.wait_ge(qn_done, b * (GB * NQ) + g * NQ + i + 1)
                        if i == 0:
                            pe.wait_ge(acc_free, b * GB + g + 1)
                        pv_half(g, i, 0)
                        scores_of(qg, qi, 3, unit + 3)
                        pv_half(g, i, 1)

        @block.scalar
        def _(act):
            act.wait_ge(s_const, 1)
            nc.scalar.activation(warm[:], warm[:], ACT.Exp).then_inc(exp_done, 1)
            act.wait_ge(s_c, 16)
            nc.scalar.activation(c_e[:], c_sb[:], ACT.Exp, scale=-1.0).then_inc(s_ce, 1)

            def evac_t(s, count):
                act.wait_ge(t_pe, count)
                for ci in range(2):
                    cc = 2 * s + ci
                    a = nc.scalar.activation(hT32[:, cc, :], pj[s][:, ci * 2 * P:(ci + 1) * 2 * P], ACT.Identity,
                                             bias=mod_now[:, CC + cc:CC + cc + 1], scale=mod_now[:, cc:cc + 1])
                a.then_inc(t_evac, 1)

            def evac_q(par, s, count):
                act.wait_ge(q_pe, count)
                for ci in range(2):
                    cc = 2 * s + ci
                    a = nc.scalar.activation(qT[par][:, cc, :], pj[s][:, ci * 2 * P:(ci + 1) * 2 * P], ACT.Identity,
                                             bias=bq_col[:, cc:cc + 1], scale=1.0 / WS)
                a.then_inc(q_evac, 1)

            def exp_unit(par, hq, count):
                act.wait_ge(max_done, count)
                nc.scalar.activation(probs[:, par, hq, :], sc[hq % 2][:], ACT.Exp, bias=nmax[:, par, hq:hq + 1],
                                     accum_out=rsum[:, par, hq:hq + 1]).then_inc(exp_done, 1)

            act.wait_ge(s_now, 1)
            evac_t(0, 1)
            evac_t(1, 2)
            act.wait_ge(s_in, 8 * 16)
            evac_q(0, 0, 1)
            evac_q(0, 1, 2)
            act.wait_ge(s_ht, 1)
            evac_t(0, 3)
            evac_t(1, 4)
            for hq in range(HG):
                exp_unit(0, hq, hq + 1)
            with act.Fori(0, B) as b:
                for g in range(GB):
                    if g == 2:
                        act.wait_ge(t_evac, b * (2 * GB) + 2 * (g + 2))
                        nc.scalar.activation(mod_now[:], mod_table[:, b + 1, :], ACT.Identity).then_inc(s_now, 1)
                    m2 = b * GB * 2 + 2 * (g + 1)
                    for i in range(NQ):
                        act.wait_ge(pv_done, b * (GB * NQ) + g * NQ + i + 1)
                        for hq in range(HG):
                            exp_unit((i + 1) % 2, hq, b * (GB * NQ * HG) + (g * NQ + i + 1) * HG + hq + 1)
                            if hq == 2 and 4 <= i < 6:
                                evac_q((g + 1) % 2, i - 4, m2 + i - 3)
                        if i >= 6:
                            if i == 6:
                                act.wait_ge(s_ht, b * GB + g + 2)
                                act.wait_ge(s_now, b + 1 + (g >= 2))
                            evac_t(i - 6, b * GB * 2 + 2 * (g + 2) + i - 5)

        @block.vector
        def _(dve):
            dve.sem_inc(acc_free, 1)
            dve.sem_inc(x2_done, 1)
            nc.vector.memset(warm[:], 0.0).then_inc(s_const, 1)
            nc.vector.memset(minus_half[:], -0.5).then_inc(s_const, 1)
            dve.wait_ge(s_ce, 1)
            nc.vector.tensor_scalar(mod_t[:, 0, :], c_e[:], 1.0, None, ALU.add).then_inc(s_v, 1)
            dve.wait_ge(s_v, 1)
            nc.vector.reciprocal(mod_t[:, 1, :], mod_t[:, 0, :]).then_inc(s_v, 1)
            dve.wait_ge(s_v, 2)
            nc.vector.tensor_tensor(c_e[:], c_sb[:], mod_t[:, 1, :], ALU.mult).then_inc(s_silu, 1)
            dve.wait_ge(s_ct, 1)
            nc.vector.tensor_copy(cT[:], pj[0][:, 0:CC * B].rearrange("p (c b) -> p c b", b=B)).then_inc(s_ctc, 1)

            def wait_alone(s, count):
                dve.wait_ge(s, count)
                dve.sem_inc(s_idle, 1)

            def stats_of_x(buf, loads, count):
                dve.wait_ge(s_x[buf], loads)
                for p in range(2):
                    st = nc.vector.bn_stats(stats1[:, p, :], xt[buf][:, p, :])
                st.then_inc(s_bn1, 1)

            def aggregate(count):
                wait_alone(s_bn1, count)
                for p in range(2):
                    st = nc.vector.bn_aggr(mv1[:, p, :], stats1[:, p, :])
                st.then_inc(s_agg1, 1)
                dve.wait_ge(s_agg1, count)
                nc.vector.tensor_scalar(var1[:], mv1[:, :, 1], EPS, None, ALU.add)
                nc.vector.tensor_scalar(nmean1[:], mv1[:, :, 0], -1.0, None, ALU.mult).then_inc(s_var1, 1)

            stats_of_x(0, 16, 1)
            aggregate(1)
            mod_banks = (sc[0][0:B, 0:D], sc[0][0:B, D:2 * D], sc[1][0:B, 0:D], sc[1][0:B, D:2 * D])
            dve.wait_ge(s_mod, 1)
            nc.vector.tensor_scalar(mod_t[:, 0, :], mod_banks[0], 1.0, None, ALU.add)
            dve.wait_ge(s_mod, 2)
            nc.vector.tensor_copy(mod_t[:, 1, :], mod_banks[1]).then_inc(s_mt, 1)
            dve.wait_ge(s_ct, 2)
            tab = pj[1][:, 0:2 * CC * B].rearrange("p (k b) -> p b k", b=B)
            nc.vector.tensor_copy(mod_table[:, B, :], tab[:, B - 1, :])
            nc.vector.tensor_copy(mod_now[:], tab[:, 0, :]).then_inc(s_now, 1)
            nc.vector.tensor_copy(mod_table[:, 0:B, :], tab).then_inc(s_table, 1)
            for k, (w16, st) in enumerate(zip((wk16, wv16, wq16), w_stage)):
                dve.wait_ge(s_w[k], 16)
                nc.vector.tensor_scalar(w16[:, 0], st, WS, None, ALU.mult).then_inc(s_wsplit, 1)
                dve.wait_ge(s_wsplit, 2 * k + 1)
                nc.vector.scalar_tensor_tensor(out=w16[:, 1], in0=st, scalar=WS, in1=w16[:, 0],
                                               op0=ALU.mult, op1=ALU.subtract).then_inc(s_wsplit, 1)
            dve.wait_ge(s_in, 8 * 16)
            nc.vector.tensor_scalar(tempw_col[:], temp_col[:], 1.0 / WS, None, ALU.mult)
            for g in range(GB):
                last = nc.vector.tensor_scalar(bkt_row[:, g, :], bk_row[:], temp_col[:, g:g + 1], None, ALU.mult)
            last.then_inc(s_v, 1)
            def kv_out(g, kk, count, free):
                dve.wait_ge(kv_pe, count)
                if free is not None:
                    dve.wait_ge(kv_split, free)
                if kk < 2:
                    nc.vector.scalar_tensor_tensor(out=kv32[kk % 2][:], in0=pj[kk % 2][:], scalar=tempw_col[:, g:g + 1],
                                                   in1=bkt_row[:, g, :], op0=ALU.mult, op1=ALU.add).then_inc(kv_evac, 1)
                else:
                    nc.vector.scalar_tensor_tensor(out=kv32[kk % 2][:], in0=pj[kk % 2][:], scalar=1.0 / WS,
                                                   in1=bv_row[:], op0=ALU.mult, op1=ALU.add).then_inc(kv_evac, 1)

            def row_max(par, hq, count):
                dve.wait_ge(score_pe, count)
                nc.vector.tensor_reduce(nmax[:, par, hq:hq + 1], sc[hq % 2][:], AX.X, ALU.max, negate=True).then_inc(max_done, 1)

            dve.wait_ge(s_v, 3)
            for kk in range(4):
                kv_out(0, kk, kk + 1, kk - 1 if kk >= 2 else None)
            dve.wait_ge(s_xhat, 1)
            stats_of_x(1, 16, 2)
            aggregate(2)
            for k, (row, add) in enumerate(((0, 0.0), (2, 0.0), (1, 1.0), (3, 0.0))):
                dve.wait_ge(s_mod, k + 3)
                last = nc.vector.tensor_scalar(mod_b[:, row, :], mod_banks[(k + 2) % 4], add, None, ALU.add)
            last.then_inc(s_modc, 1)
            dve.wait_ge(s_modc, 1)
            v = 3
            for row in (0, 3):
                gate = mod_b[:, row, :]
                nc.vector.tensor_scalar(sign, gate, 0.0, 2.0, ALU.is_ge, ALU.mult).then_inc(s_v, 1)
                nc.vector.scalar_tensor_tensor(out=size, in0=gate, scalar=-1.0, in1=gate, op0=ALU.mult, op1=ALU.max).then_inc(s_v, 1)
                dve.wait_ge(s_v, v + 2)
                nc.vector.tensor_scalar(sign, sign, -1.0, None, ALU.add).then_inc(s_v, 1)
                dve.wait_ge(s_v, v + 3)
                nc.vector.scalar_tensor_tensor(out=gate, in0=size, scalar=GATE_MIN, in1=sign,
                                               op0=ALU.max, op1=ALU.mult).then_inc(s_v, 1)
                dve.wait_ge(s_v, v + 4)
                v += 4
            nc.vector.tensor_copy(size, sign).then_inc(s_modv, 1)
            for hq in range(HG):
                row_max(0, hq, hq + 1)

            def dot_router(p, b, g):
                nc.vector.scalar_tensor_tensor(out=dot_out[:, p], in0=hbuf[:, (g + 1) % 2, p, :], scalar=1.0, in1=router_row[:],
                                               op0=ALU.mult, op1=ALU.mult,
                                               accum_out=scores[:, bass.ds(b * (2 * GB) + 2 * g + p, 1)]).then_inc(s_dot, 1)

            with dve.Fori(0, B) as b:
                for g in range(GB):
                    m4 = b * GB * 4 + 4 * (g + 1)
                    for i in range(NQ):
                        par = (i + 1) % 2
                        unit = b * (GB * NQ * HG) + (g * NQ + i + 1) * HG
                        quad = b * (GB * NQ) + g * NQ + i + 1
                        row_max(par, 0, unit + 1)
                        row_max(par, 1, unit + 2)
                        dve.wait_ge(exp_done, unit + 1)
                        nc.vector.reciprocal(rinv[:, i % 2, :], rsum[:, i % 2, :]).then_inc(inv_done, 1)
                        if i == 0:
                            dve.wait_ge(q_evac, b * (2 * GB) + 2 * (g + 1))
                        dve.wait_ge(inv_done, quad)
                        nc.vector.tensor_tensor(
                            qn[:, i % 2], qT[g % 2][:, i % CC, (i // CC) * P:(i // CC + 1) * P].rearrange("p (h j) -> p h j", j=DH),
                            rinv[:, i % 2, :].unsqueeze(2).broadcast_to([P, HG, DH]), ALU.mult).then_inc(qn_done, 1)
                        if i == 0:
                            dve.wait_ge(s_xhat, b * GB + g + 2)
                            stats_of_x((g + 2) % 4, b * 16 + 16 * ((g + 2) // 4 + 1), b * GB + g + 3)
                        if i == 1:
                            aggregate(b * GB + g + 3)
                        if i == 4 or i == 5:
                            dve.wait_ge(post_done, b * GB + g + 1)
                            dot_router(i - 4, b, g)
                        row_max(par, 2, unit + 3)
                        row_max(par, 3, unit + 4)
                        if i < 4:
                            kv_out((g + 1) % GB, i, m4 + i + 1, m4 + i - 1)
                    n1 = b * GB + g + 1
                    dve.wait_ge(pv_done, b * (GB * NQ) + (g + 1) * NQ + 1)
                    dve.wait_ge(s_rows, b * 64 + 64)
                    nc.vector.tensor_tensor(x2[:], acc[:].rearrange("q (p n) -> q p n", p=2),
                                            rows[:, 0:1, :].broadcast_to([P, 2, D]), ALU.mult).then_inc(acc_free, 1)
                    dve.wait_ge(acc_free, n1 + 1)
                    nc.vector.tensor_tensor(x2[:], x2[:], xt[g][:], ALU.add).then_inc(x2_done, 1)
                    dve.wait_ge(x2_done, n1 + 1)
                    for p in range(2):
                        st = nc.vector.bn_stats(stats2[:, p, :], x2[:, p, :])
                    st.then_inc(s_bn2, 1)
                    wait_alone(s_bn2, n1)
                    for p in range(2):
                        st = nc.vector.bn_aggr(mv2[:, p, :], stats2[:, p, :])
                    st.then_inc(s_agg2, 1)
                    dve.wait_ge(s_agg2, n1)
                    nc.vector.tensor_scalar(var2[:], mv2[:, :, 1], EPS, None, ALU.add)
                    nc.vector.tensor_scalar(nmean2[:], mv2[:, :, 0], -1.0, None, ALU.mult).then_inc(s_var2, 1)
            dve.wait_ge(post_done, NG + 1)
            for p in range(2):
                dot_router(p, B, 0)
            dve.wait_ge(s_dot, 2 * NG + 2)

        @block.gpsimd
        def _(pool):
            pool.sem_inc(post_done, 1)
            nc.gpsimd.memset(ident[:], 0.0).then_inc(s_id, 1)
            pool.wait_ge(s_id, 1)
            nc.gpsimd.affine_select(out=ident[:], in_=ident[:], compare_op=ALU.not_equal, fill=1.0, base=0,
                                    pattern=[[-1, P]], channel_multiplier=1).then_inc(s_id, 1)
            pool.wait_ge(s_const, 2)

            def wait_alone(s, count):
                pool.wait_ge(s, count)
                pool.sem_inc(s_idle, 1)

            def normed(dst, src, var, nmean, rstd, s_var, s_r, s_out, count):
                pool.wait_ge(s_var, count)
                nc.gpsimd.tensor_tensor(rstd[:], var[:], minus_half[:], ALU.pow).then_inc(s_r, 1)
                wait_alone(s_r, count)
                for p in range(2):
                    last = nc.gpsimd.tensor_scalar(dst[:, p, :], src[:, p, :], nmean[:, p:p + 1], rstd[:, p:p + 1], ALU.add, ALU.mult)
                last.then_inc(s_out, 1)

            def split_hT(count, t_count):
                wait_alone(t_evac, t_count)
                nc.gpsimd.tensor_copy(hT16[:, 0], hT32[:]).then_inc(s_hi, 1)
                pool.wait_ge(s_hi, count)
                nc.gpsimd.tensor_tensor(hT16[:, 1], hT32[:], hT16[:, 0], ALU.subtract).then_inc(s_ht, 1)

            def split_kv(kk, count):
                dst = (k16, v16)[kk // 2][:, :, (kk % 2) * D:(kk % 2 + 1) * D]
                wait_alone(kv_evac, count)
                nc.gpsimd.tensor_copy(dst[:, 0], kv32[kk % 2][:]).then_inc(kv_hi, 1)
                pool.wait_ge(kv_hi, count)
                nc.gpsimd.tensor_tensor(dst[:, 1], kv32[kk % 2][:], dst[:, 0], ALU.subtract).then_inc(kv_split, 1)

            normed(xhat, xt[0], var1, nmean1, rstd1, s_var1, s_r1, s_xhat, 1)
            split_hT(1, 2)
            pool.wait_ge(s_wsplit, 6)
            nc.gpsimd.memset(hbuf[:, 1], 0.0)
            for kk in range(4):
                split_kv(kk, kk + 1)
            pool.wait_ge(t_pe, 2)
            normed(xhat, xt[1], var1, nmean1, rstd1, s_var1, s_r1, s_xhat, 2)
            split_hT(2, 4)
            with pool.Fori(0, B) as b:
                for g in range(GB):
                    m4 = b * GB * 4 + 4 * (g + 1)
                    n3 = b * GB + g + 3
                    for kk in range(4):
                        split_kv(kk, m4 + kk + 1)
                        if kk == 1:
                            pool.wait_ge(t_pe, b * (2 * GB) + 2 * (g + 2))
                            normed(xhat, xt[(g + 2) % 4], var1, nmean1, rstd1, s_var1, s_r1, s_xhat, n3)
                    split_hT(n3, b * (2 * GB) + 2 * (g + 3))
                    n1 = b * GB + g + 1
                    pool.wait_ge(s_st[g % 2], b * (32 * GB // 2) + 32 * (g // 2) + 16)
                    normed(xhat2, x2, var2, nmean2, rstd2, s_var2, s_r2, s_xh2, n1)
                    h, bs = hbuf[:, g % 2], base[:, g % 2]
                    steps = ((h, xhat2[:], 1, ALU.mult), (h, h, 2, ALU.add), (bs, h, 3, ALU.mult))
                    pool.wait_ge(s_xh2, n1)
                    for k, (dst, a, row, op) in enumerate(steps):
                        nc.gpsimd.tensor_tensor(dst, a, rows[:, row:row + 1, :].broadcast_to([P, 2, D]), op).then_inc(s_hm, 1)
                        pool.wait_ge(s_hm, b * (3 * GB) + 3 * g + k + 1)
                    nc.gpsimd.tensor_tensor(bs, bs, x2[:], ALU.add).then_inc(post_done, 1)


def ffn_phase(nc, W1, b1, W2, b2, out, h_rows, sel_rows, mod_rows, scores):
    out_rows = out.rearrange("b t d -> (b t) d")
    sel_b = sel_rows.rearrange("(b k s) w -> b s k w", b=B, s=P)
    TB = 2 * GB
    KT = KEEP // P
    PAD = (GB - 1) * 2 * P

    with ExitStack() as ctx:
        def sb(name, shape, dt):
            return ctx.enter_context(nc.sbuf_tensor(name, shape, dt))

        def pb(name, shape):
            return ctx.enter_context(nc.psum_tensor(name, shape, F32))

        def sem(name):
            return ctx.enter_context(nc.semaphore(name))

        w1_16 = sb("w1_16", [P, 2, CC, F], F16)
        w2_16 = sb("w2_16", [P, 2, FC, D], F16)
        stage = sb("stage", [P, 4, 4, D], F32)
        b1_col = sb("b1_col", [P, FC], F32)
        b2_row = sb("b2_row", [P, D], F32)
        gb_row = sb("gb_row", [P, 2, D], F32)
        id2 = sb("id2", [P, P], F32)
        ones = sb("ones", [P, P], F32)
        earlier = sb("earlier", [P, 2, PAD + 2 * P + PAD], BF16)
        tok_i = sb("tok_i", [P, B * TB], I32)
        e_neg = sb("e_neg", [P, B * TB], F32)
        tokens = sb("tokens", [P, B * TB, 2], F32)
        warm2 = sb("warm2", [P, 1], F32)
        s8 = sb("s8", [P, TB], F32)
        diag = sb("diag", [P, TB, P], F32)
        srow = sb("srow", [P, TB, P], F32)
        scol = sb("scol", [P, TB], F32)
        cmp_out = sb("cmp_out", [P, 2, TB * P], BF16)
        above = sb("above", [P, TB], F32)
        ties = sb("ties", [P, TB], F32)
        rank = sb("rank", [P, TB], F32)
        drop = sb("drop", [P, TB], F32)
        first = sb("first", [P, 1], F32)
        slot = sb("slot", [P, TB], I32)
        tok8 = sb("tok8", [P, TB, 2], F32)
        kept = sb("kept", [P, 2, KT, 2], F32)
        kept_i = sb("kept_i", [P, 2, KT], I32)
        hs = sb("hs", [P, 2, KT, D], F32)
        bs = sb("bs", [P, 2, KT, D], F32)
        fT16 = sb("fT16", [P, 2, 2, CC, KEEP], F16)
        g32 = sb("g32", [P, 2, KEEP], F32)
        g16 = sb("g16", [P, 2, 2, KEEP], F16)
        y = sb("y", [P, 2, KT, D], F32)

        acc = [pb(f"ff2_{k}", [P, D]) for k in range(KT)]
        ff = [pb(f"ff1_{k}", [P, KEEP]) for k in range(2)]
        aux = [pb(f"aux{k}", [P, D]) for k in range(2)]

        s_stage = [sem(f"s_stage{i}") for i in range(8)]
        s_b = sem("s_b")
        s_gb = [sem(f"s_gb{i}") for i in range(2)]
        w_hi = sem("w_hi")
        w_lo = sem("w_lo")
        s_idle = sem("s_idle2")
        s_c2 = sem("s_c2")
        s_e = sem("s_e")
        s_d = sem("s_d")
        s_s8 = sem("s_s8")
        s_diag = sem("s_diag")
        s_bc = sem("s_bc")
        s_srow = sem("s_srow")
        s_ext = sem("s_ext")
        s_cmp = sem("s_cmp")
        s_rank = sem("s_rank")
        s_slot = sem("s_slot")
        s_sel = sem("s_sel")
        s_kept = [sem(f"s_kept{i}") for i in range(2)]
        s_ids = sem("s_ids")
        s_gh = [sem(f"s_gh{i}") for i in range(2)]
        s_gbs = [sem(f"s_gbs{i}") for i in range(2)]
        ft_pe = sem("ft_pe")
        ft_hi = sem("ft_hi")
        ft_lo = sem("ft_lo")
        ff1_pe = sem("ff1_pe")
        gelu_done = sem("gelu_done")
        g_hi = sem("g_hi")
        g_split = sem("g_split")
        ff2_pe = sem("ff2_pe")
        acc_out = sem("acc_out")
        y_gb = sem("y_gb")
        y_done = sem("y_done")
        s_out = [sem(f"s_out{i}") for i in range(2)]

        block = ctx.enter_context(nc.Block())

        def batches(eng, body):
            with eng.Fori(0, B // 2 - 1) as bb:
                for par in range(2):
                    body(bb, par, False)
            for par in range(2):
                body(B // 2 - 1, par, par == 1)

        def n_of(bb, par, per, off):
            return bb * (2 * per) + (per * par + off)

        @block.sync
        def _(sp):
            def load_kept(bb, par):
                with nc.allow_non_contiguous_dma(reason="number and weight of 512 tokens"):
                    sp.wait_ge(s_sel, n_of(bb, par, 16 * TB, 16 * TB))
                    sp.dma_start(kept[:, par], sel_b[bb * 2 + par]).then_inc(s_kept[par], 16)

            for j in range(8):
                if j == 7:
                    load_kept(0, 0)
                if j < 4:
                    src = W1[:, j * D:(j + 1) * D].rearrange("(c p) n -> p c n", p=P)
                else:
                    src = W2[(j - 4) * 4 * P:(j - 3) * 4 * P, :].rearrange("(k p) n -> p k n", p=P)
                    sp.wait_ge(w_lo, j - 3)
                sp.dma_start(stage[:, j % 4], src).then_inc(s_stage[j], 16)
                if j == 3:
                    sp.dma_start(b2_row[:], b2.partition_broadcast(P)).then_inc(s_b, 16)
                    with nc.allow_non_contiguous_dma(reason="2048 biases, once"):
                        sp.dma_start(b1_col[:], b1.rearrange("(f p) -> p f", p=P)).then_inc(s_b, 16)

            def body(bb, par, last):
                sp.wait_ge(y_done, n_of(bb, par, KT, 0) + 1)
                sp.dma_start(gb_row[:, par], mod_rows[bb * 2 + par, 3].partition_broadcast(P)).then_inc(s_gb[par], 16)
                if not last:
                    load_kept(bb + (par == 1), 1 - par)

            batches(sp, body)
            for i in range(2):
                sp.wait_ge(s_out[i], 16 * KT * B // 2)

        @block.tensor
        def _(pe):
            def broadcast_scores(bb, par):
                pe.wait_ge(s_diag, n_of(bb, par, 1, 1))
                for k in range(2):
                    mm = nc.tensor.matmul(aux[k][:], ones[:], diag[:, k * TB // 2:(k + 1) * TB // 2, :], start=True, stop=True)
                mm.then_inc(s_bc, 1)

            def transpose_kept(bb, par, cc):
                if cc == 0:
                    pe.wait_ge(s_gh[par], bb * (16 * KT) + 16 * KT)
                    pe.wait_ge(s_srow, n_of(bb, par, 1, 1))
                if cc >= 2:
                    pe.wait_ge(ft_lo, n_of(bb, par, CC, cc - 1))
                for kt in range(KT):
                    mm = nc.tensor.transpose(aux[cc % 2][:, kt * P:(kt + 1) * P], hs[:, par, kt, cc * P:(cc + 1) * P], id2[:])
                mm.then_inc(ft_pe, 1)

            def ff1(bb, par, f):
                pe.wait_ge(gelu_done, n_of(bb, par, FC, f + 1))
                if f % 4 == 0:
                    pe.wait_ge(w_lo, f // 4 + 1)
                terms = [(cc, a, z) for cc in range(CC) for z, a in ((0, 0), (0, 1), (1, 0))]
                for t, (cc, a, z) in enumerate(terms):
                    mm = nc.tensor.matmul(ff[f % 2][:], w1_16[:, z, cc, f * P:(f + 1) * P], fT16[:, par, a, cc, :],
                                          start=(t == 0), stop=(t == len(terms) - 1))
                mm.then_inc(ff1_pe, 1)

            def ff2(bb, par, f):
                if f % 4 == 0:
                    pe.wait_ge(w_lo, 4 + f // 4 + 1)
                if f == 0:
                    pe.wait_ge(acc_out, n_of(bb, par, KT, 0) + 1)
                pe.wait_ge(g_split, n_of(bb, par, FC, f + 3))
                for kt in range(KT):
                    for t, (a, z) in enumerate(((0, 0), (0, 1), (1, 0))):
                        mm = nc.tensor.matmul(acc[kt][:], g16[:, f % 2, a, kt * P:(kt + 1) * P], w2_16[:, z, f, :],
                                              start=(f == 0 and t == 0), stop=(f == FC - 1 and t == 2))
                mm.then_inc(ff2_pe, 1)

            pe.wait_ge(s_c2, 3)
            broadcast_scores(0, 0)
            for cc in range(CC):
                transpose_kept(0, 0, cc)

            def body(bb, par, last):
                pe.wait_ge(ft_lo, n_of(bb, par, CC, CC))
                for f in range(FC):
                    ff1(bb, par, f)
                    if f >= 1:
                        ff2(bb, par, f - 1)
                    if not last and f == 1:
                        broadcast_scores(bb + (par == 1), 1 - par)
                    if not last and f >= FC - CC:
                        transpose_kept(bb + (par == 1), 1 - par, f - (FC - CC))
                ff2(bb, par, FC - 1)

            batches(pe, body)

        @block.scalar
        def _(act):
            nc.scalar.activation(e_neg[:], scores[:, 2:], ACT.Exp, scale=-1.0).then_inc(s_e, 1)

            def high_part(j):
                act.wait_ge(s_stage[j], 16)
                if j < 4:
                    dst = w1_16[:, 0, :, j * D:(j + 1) * D]
                else:
                    dst = w2_16[:, 0, 4 * (j - 4):4 * (j - 3), :]
                nc.scalar.activation(dst, stage[:, j % 4], ACT.Identity, scale=WS).then_inc(w_hi, 1)

            def copy_scores(bb, par):
                act.wait_ge(s_bc, n_of(bb, par, 1, 1))
                for k in range(2):
                    a = nc.scalar.activation(srow[:, k * TB // 2:(k + 1) * TB // 2, :].rearrange("p a b -> p (a b)"), aux[k][:], ACT.Identity)
                a.then_inc(s_srow, 1)

            def kept_high(bb, par, cc):
                act.wait_ge(ft_pe, n_of(bb, par, CC, cc + 1))
                nc.scalar.activation(fT16[:, par, 0, cc, :], aux[cc % 2][:], ACT.Identity).then_inc(ft_hi, 1)

            for j in range(2):
                high_part(j)
            copy_scores(0, 0)
            for j in range(2, 8):
                high_part(j)
            act.wait_ge(s_d, 1)
            nc.scalar.activation(warm2[:], warm2[:], ACT.Gelu_apprx_tanh).then_inc(gelu_done, 2)
            for cc in range(CC):
                kept_high(0, 0, cc)
            act.wait_ge(s_b, 32)

            def body(bb, par, last):
                for f in range(FC):
                    act.wait_ge(g_split, n_of(bb, par, FC, f + 1))
                    act.wait_ge(ff1_pe, n_of(bb, par, FC, f + 1))
                    nc.scalar.activation(g32[:, f % 2, :], ff[f % 2][:], ACT.Gelu_apprx_tanh, bias=b1_col[:, f:f + 1],
                                         scale=1.0 / WS).then_inc(gelu_done, 1)
                    if not last and f == 2:
                        copy_scores(bb + (par == 1), 1 - par)
                    if not last and f > FC - CC:
                        kept_high(bb + (par == 1), 1 - par, f - (FC - CC) - 1)
                if not last:
                    kept_high(bb + (par == 1), 1 - par, CC - 1)

            batches(act, body)

        @block.vector
        def _(dve):
            dve.sem_inc(acc_out, 1)
            dve.sem_inc(y_done, 1)
            nc.vector.memset(warm2[:], 0.0).then_inc(s_d, 1)
            nc.vector.memset(first[:], 0.0)
            nc.vector.memset(g16[:, 0, 0, 0:2], 0.0).then_inc(g_split, 2)
            dve.wait_ge(s_c2, 3)

            def low_part(j):
                dve.wait_ge(w_hi, j + 1)
                if j < 4:
                    hi, lo = (w1_16[:, z, :, j * D:(j + 1) * D] for z in range(2))
                else:
                    hi, lo = (w2_16[:, z, 4 * (j - 4):4 * (j - 3), :] for z in range(2))
                nc.vector.scalar_tensor_tensor(out=lo, in0=stage[:, j % 4], scalar=WS, in1=hi, op0=ALU.mult,
                                               op1=ALU.subtract).then_inc(w_lo, 1)

            def diagonals(bb, par):
                nc.vector.tensor_copy(s8[:], scores[:, bass.ds(bb * (2 * TB) + par * TB + 2, TB)]).then_inc(s_s8, 1)
                dve.wait_ge(s_s8, n_of(bb, par, 1, 1))
                nc.vector.tensor_tensor(diag[:], id2[:].unsqueeze(1).broadcast_to([P, TB, P]),
                                        s8[:].unsqueeze(2).broadcast_to([P, TB, P]), ALU.mult).then_inc(s_diag, 1)

            def own_scores(bb, par):
                dve.wait_ge(s_srow, n_of(bb, par, 1, 1))
                nc.vector.tensor_tensor(diag[:], srow[:], id2[:].unsqueeze(1).broadcast_to([P, TB, P]), ALU.mult).then_inc(s_ext, 1)
                dve.wait_ge(s_ext, n_of(bb, par, 2, 1))
                nc.vector.tensor_reduce(scol[:], diag[:], AX.X, ALU.add).then_inc(s_ext, 1)
                dve.wait_ge(s_ext, n_of(bb, par, 2, 2))

            def count_above(bb, par, t):
                flat = srow[:].rearrange("p a b -> p (a b)")
                if t >= 1:
                    dve.wait_ge(s_cmp, n_of(bb, par, 2 * TB, 2 * t - 1))
                nc.vector.tensor_scalar(cmp_out[:, 0], flat, scol[:, t:t + 1], 0.0, ALU.is_gt, ALU.add,
                                        accum_out=above[:, t:t + 1]).then_inc(s_cmp, 1)
                if t >= 1:
                    dve.wait_ge(s_cmp, n_of(bb, par, 2 * TB, 2 * t))
                at = PAD - (t // 2) * 2 * P
                nc.vector.scalar_tensor_tensor(out=cmp_out[:, 1], in0=flat, scalar=scol[:, t:t + 1],
                                               in1=earlier[:, t % 2, at:at + TB * P], op0=ALU.is_equal, op1=ALU.mult,
                                               accum_out=ties[:, t:t + 1]).then_inc(s_cmp, 1)

            def slots(bb, par):
                dve.wait_ge(s_cmp, n_of(bb, par, 2 * TB, 2 * TB))
                nc.vector.tensor_tensor(rank[:], above[:], ties[:], ALU.add).then_inc(s_rank, 1)
                dve.wait_ge(s_rank, n_of(bb, par, 3, 1))
                nc.vector.tensor_scalar(drop[:], rank[:], float(KEEP), BIG, ALU.is_ge, ALU.mult).then_inc(s_rank, 1)
                dve.wait_ge(s_rank, n_of(bb, par, 3, 2))
                nc.vector.tensor_copy(tok8[:], tokens[:, bass.ds(bb * (2 * TB) + par * TB, TB), :])
                nc.vector.scalar_tensor_tensor(out=slot[:], in0=rank[:], scalar=first[:, 0:1], in1=drop[:],
                                               op0=ALU.add, op1=ALU.add).then_inc(s_slot, 1)
                nc.vector.tensor_scalar(first[:], first[:], float(KEEP), None, ALU.add).then_inc(s_rank, 1)
                dve.wait_ge(s_rank, n_of(bb, par, 3, 3))

            def numbers(bb, par):
                dve.wait_ge(s_kept[par], bb * 16 + 16)
                nc.vector.tensor_copy(kept_i[:, par], kept[:, par, :, 0]).then_inc(s_ids, 1)

            def kept_low(bb, par, cc):
                dve.wait_ge(ft_hi, n_of(bb, par, CC, cc + 1))
                nc.vector.tensor_tensor(fT16[:, par, 1, cc, :], aux[cc % 2][:], fT16[:, par, 0, cc, :], ALU.subtract).then_inc(ft_lo, 1)

            dve.wait_ge(s_e, 1)
            nc.vector.tensor_scalar(e_neg[:], e_neg[:], 1.0, None, ALU.add).then_inc(s_d, 1)
            dve.wait_ge(s_d, 2)
            nc.vector.reciprocal(tokens[:, :, 1], e_neg[:]).then_inc(s_d, 1)
            nc.vector.tensor_copy(tokens[:, :, 0], tok_i[:]).then_inc(s_d, 1)
            dve.wait_ge(s_d, 4)
            diagonals(0, 0)
            low_part(0)
            own_scores(0, 0)
            for t in range(TB):
                count_above(0, 0, t)
            slots(0, 0)
            low_part(1)
            low_part(2)
            numbers(0, 0)
            for j in range(3, 8):
                low_part(j)
            for cc in range(CC):
                kept_low(0, 0, cc)

            def body(bb, par, last):
                nb, npar = bb + (par == 1), 1 - par
                for f in range(FC):
                    dve.wait_ge(gelu_done, n_of(bb, par, FC, f + 3))
                    nc.vector.tensor_copy(g16[:, f % 2, 0, :], g32[:, f % 2, :]).then_inc(g_hi, 1)
                    dve.wait_ge(g_hi, n_of(bb, par, FC, f + 1))
                    nc.vector.tensor_tensor(g16[:, f % 2, 1, :], g32[:, f % 2, :], g16[:, f % 2, 0, :], ALU.subtract).then_inc(g_split, 1)
                    if last:
                        continue
                    if f == 0:
                        diagonals(nb, npar)
                    if f == 3:
                        own_scores(nb, npar)
                    if 4 <= f < 8:
                        count_above(nb, npar, 2 * (f - 4))
                        count_above(nb, npar, 2 * (f - 4) + 1)
                    if f == 7:
                        slots(nb, npar)
                    if f == 10:
                        numbers(nb, npar)
                    if f > FC - CC:
                        kept_low(nb, npar, f - (FC - CC) - 1)
                dve.wait_ge(ff2_pe, n_of(bb, par, FC, FC))
                dve.wait_ge(s_b, 32)
                for kt in range(KT):
                    nc.vector.scalar_tensor_tensor(out=y[:, par, kt, :], in0=acc[kt][:], scalar=1.0 / WS, in1=b2_row[:],
                                                   op0=ALU.mult, op1=ALU.add).then_inc(acc_out, 1)
                if not last:
                    kept_low(nb, npar, CC - 1)
                for kt in range(KT):
                    if kt == 0:
                        dve.wait_ge(s_gbs[par], bb * (16 * KT) + 16 * KT)
                    dve.wait_ge(y_gb, n_of(bb, par, KT, kt + 1))
                    nc.vector.scalar_tensor_tensor(out=y[:, par, kt, :], in0=y[:, par, kt, :], scalar=kept[:, par, kt, 1:2],
                                                   in1=bs[:, par, kt, :], op0=ALU.mult, op1=ALU.add).then_inc(y_done, 1)

            batches(dve, body)

        @block.gpsimd
        def _(pool):
            nc.gpsimd.memset(id2[:], 0.0).then_inc(s_c2, 1)
            nc.gpsimd.memset(ones[:], 1.0)
            for p in range(2):
                nc.gpsimd.memset(earlier[:, p, 0:PAD + 2 * P], 1.0)
                last_one = nc.gpsimd.memset(earlier[:, p, PAD + 2 * P:], 0.0)
            nc.gpsimd.iota(tok_i[:], pattern=[[2 * P, NG], [1, 2]], base=0, channel_multiplier=2).then_inc(s_c2, 1)
            pool.wait_ge(s_c2, 2)
            for p in range(2):
                for pp in range(2):
                    part = earlier[:, p, PAD + pp * P:PAD + (pp + 1) * P]
                    nc.gpsimd.affine_select(out=part, in_=part, compare_op=ALU.is_ge if p > pp else ALU.is_gt, fill=0.0, base=0,
                                            pattern=[[-1, P]], channel_multiplier=1)
            nc.gpsimd.affine_select(out=id2[:], in_=id2[:], compare_op=ALU.not_equal, fill=1.0, base=0,
                                    pattern=[[-1, P]], channel_multiplier=1).then_inc(s_c2, 1)

            def wait_alone(s, count):
                pool.wait_ge(s, count)
                pool.sem_inc(s_idle, 1)

            def store_kept(bb, par):
                wait_alone(s_slot, n_of(bb, par, 1, 1))
                for t in range(TB):
                    nc.gpsimd.indirect_dma_start(sel_rows, bass.IndirectOffsetOnAxis(slot[:, t:t + 1], 0), tok8[:, t, :], None,
                                                 bounds_check=B * KEEP - 1, oob_is_err=False).then_inc(s_sel, 16)

            def gather(bb, par):
                wait_alone(s_ids, n_of(bb, par, 1, 1))
                for kt in range(KT):
                    nc.gpsimd.indirect_dma_start(hs[:, par, kt, :], None, h_rows,
                                                 bass.IndirectOffsetOnAxis(kept_i[:, par, kt:kt + 1], 0)).then_inc(s_gh[par], 16)
                for kt in range(KT):
                    nc.gpsimd.indirect_dma_start(bs[:, par, kt, :], None, out_rows,
                                                 bass.IndirectOffsetOnAxis(kept_i[:, par, kt:kt + 1], 0)).then_inc(s_gbs[par], 16)

            store_kept(0, 0)
            gather(0, 0)

            def body(bb, par, last):
                if not last:
                    store_kept(bb + (par == 1), 1 - par)
                    gather(bb + (par == 1), 1 - par)
                pool.wait_ge(s_gb[par], bb * 16 + 16)
                for kt in range(KT):
                    pool.wait_ge(acc_out, n_of(bb, par, KT, kt + 1) + 1)
                    nc.gpsimd.tensor_tensor(y[:, par, kt, :], y[:, par, kt, :], gb_row[:, par], ALU.mult).then_inc(y_gb, 1)
                for kt in range(KT):
                    wait_alone(y_done, n_of(bb, par, KT, kt + 1) + 1)
                    nc.gpsimd.indirect_dma_start(out_rows, bass.IndirectOffsetOnAxis(kept_i[:, par, kt:kt + 1], 0), y[:, par, kt, :],
                                                 None).then_inc(s_out[par], 16)
                wait_alone(s_out[par], bb * (16 * KT) + 16 * KT)

            batches(pool, body)


def bass_adaln_block(nc, x, Wq, bq, Wk, bk, Wv, bv, temperature, w_router, W1, b1, W2, b2, c, wmod, out):
    h_rows = nc.dram_tensor("h_rows", (B * T, D), F32, kind="Internal").ap()
    mod_rows = nc.dram_tensor("mod_rows", (B, 4, D), F32, kind="Internal").ap()
    sel_rows = nc.dram_tensor("sel_rows", (B * KEEP, 2), F32, kind="Internal").ap()
    with nc.sbuf_tensor("scores", [P, 2 * NG + 2], F32) as scores:
        attention_phase(nc, x, (Wq, Wk, Wv), (bq, bk, bv), temperature, w_router, c, wmod, out, h_rows, mod_rows, scores)
        ffn_phase(nc, W1, b1, W2, b2, out, h_rows, sel_rows, mod_rows, scores)


_INS = ['L0_attn_x', 'L0_attn_Wq', 'L0_attn_bq', 'L0_attn_Wk', 'L0_attn_bk', 'L0_attn_Wv', 'L0_attn_bv', 'L0_attn_temperature',
        'L0_ffn_w_router', 'L0_ffn_W1', 'L0_ffn_b1', 'L0_ffn_W2', 'L0_ffn_b2', 'L0_c', 'L0_wmod']


def kernel(**inputs):
    import numpy as _np
    import concourse.bacc as _bacc
    from concourse import mybir as _mybir
    from concourse.bass_utils import run_bass_kernel_spmd as _run

    nc = _bacc.Bacc("TRN2", target_bir_lowering=False, num_devices=1)
    arrays, args = {}, []
    for name in _INS:
        a = _np.ascontiguousarray(inputs[name])
        arrays[f"in_{name}"] = a
        args.append(nc.dram_tensor(f"in_{name}", a.shape, _mybir.dt.from_np(a.dtype), kind="ExternalInput").ap())
    args.append(nc.dram_tensor("out_0", (B, T, D), F32, kind="ExternalOutput").ap())
    bass_adaln_block(nc, *args)
    r = _run(nc, [arrays], core_ids=[0])
    return r.results[0]["out_0"]
```

```python
from contextlib import ExitStack

import concourse.bass as bass
from concourse import mybir

P = 128
B, T, D = 8, 1024, 512
H = 16
DH = D // H
F = 2048
KEEP = T // 2
CC = D // P
FC = F // P
HG = P // DH
TG = HG * DH * 2
GB = T // TG
NG = B * GB
NQ = T // P
WS = 64.0
QN_AFTER = 0
EPS = 1e-5
RING = 5
BIG = 1.0e6
GATE_MIN = 0.25

ALU = mybir.AluOpType
ACT = mybir.ActivationFunctionType
AX = mybir.AxisListType
F32 = mybir.dt.float32
F16 = mybir.dt.float16
BF16 = mybir.dt.bfloat16
I32 = mybir.dt.int32


def attention_phase(nc, x, w_qkv, b_qkv, temperature, w_router, c, w_mod, out, h_rows, mod_rows, scores):
    Wq, Wk, Wv = w_qkv
    bq, bk, bv = b_qkv
    x_g = x.rearrange("b (g q p) d -> (b g) q p d", g=GB, p=2)
    out_g = out.rearrange("b (g q p) d -> (b g) q p d", g=GB, p=2)
    h_g = h_rows.rearrange("(n q p) d -> n q p d", n=NG, p=2)

    with ExitStack() as ctx:
        def sb(name, shape, dt):
            return ctx.enter_context(nc.sbuf_tensor(name, shape, dt))

        def pb(name, shape):
            return ctx.enter_context(nc.psum_tensor(name, shape, F32))

        def sem(name):
            return ctx.enter_context(nc.semaphore(name))

        wq16 = sb("wq16", [P, 2, CC, D], F16)
        wk16 = sb("wk16", [P, 2, CC, D], F16)
        wv16 = sb("wv16", [P, 2, CC, D], F16)
        ident = sb("ident", [P, P], F32)
        bq_col = sb("bq_col", [P, CC], F32)
        bias16 = sb("bias16", [2 * DH, 2, D], F16)
        ones16 = sb("ones16", [2 * DH, P], F16)
        router_row = sb("router_row", [P, D], F32)
        temp_col = sb("temp_col", [P, GB], F32)
        tempw_col = sb("tempw_col", [P, GB], F32)
        mod_table = sb("mod_table", [P, B + 1, 2 * CC], F32)
        mod_now = sb("mod_now", [P, 2 * CC], F32)
        rows = sb("rows", [P, 4, D], F32)
        minus_half = sb("minus_half", [P, 2], F32)
        warm = sb("warm", [P, 1], F32)
        xt = [sb(f"xt{i}", [P, 2, D], F32) for i in range(4)]
        xhat = sb("xhat", [P, 2, D], F32)
        stats1 = sb("stats1", [P, 2, 6], F32)
        mv1 = sb("mv1", [P, 2, 2], F32)
        var1 = sb("var1", [P, 2], F32)
        nmean1 = sb("nmean1", [P, 2], F32)
        rstd1 = sb("rstd1", [P, 2], F32)
        hT32 = sb("hT32", [P, CC, 2 * P], F32)
        hT16 = [sb(f"hT16_{i}", [P, 2, CC, 2 * P], F16) for i in range(2)]
        kv32 = [sb(f"kv32_{i}", [P, D], F32) for i in range(2)]
        k16 = sb("k16", [P, 2, 2 * D], F16)
        v16 = sb("v16", [P, 2, 2 * D], F16)
        stacks = [sb(f"stacks{i}", [P, 2, HG, 2 * D], F16) for i in range(2)]
        qT = [sb(f"qT{i}", [P, CC, 2 * P], F32) for i in range(2)]
        qn = sb("qn", [P, 2, HG, DH], F32)
        probs = sb("probs", [P, 2, HG, T], F32)
        nmax = sb("nmax", [P, 2, HG], F32)
        rsum = sb("rsum", [P, 2, HG], F32)
        nhalf = sb("nhalf", [P, 2], F32)
        rhalf = sb("rhalf", [P, 2], F32)
        rinv = sb("rinv", [P, 2, HG], F32)
        x2 = sb("x2", [P, 2, D], F32)
        stats2 = sb("stats2", [P, 2, 6], F32)
        mv2 = sb("mv2", [P, 2, 2], F32)
        var2 = sb("var2", [P, 2], F32)
        nmean2 = sb("nmean2", [P, 2], F32)
        rstd2 = sb("rstd2", [P, 2], F32)
        hbuf = sb("hbuf", [P, 2, 2, D], F32)
        base = sb("base", [P, 2, 2, D], F32)
        dot_out = sb("dot_out", [P, 2, D], F32)
        c_sb = sb("c_sb", [B, D], F32)
        c_e = sb("c_e", [B, D], F32)
        cT = sb("cT", [P, CC, B], F32)
        mod_b = sb("mod_b", [B, 4, D], F32)
        mod_t = sb("mod_t", [B, 2, D], F32)
        sign = sb("sign", [B, D], F32)[:]
        size = sb("size", [B, D], F32)[:]

        acc = pb("acc", [P, 2 * D])
        sc = pb("sc", [P, RING, D])
        pj = pb("pj", [P, D])

        s_c = sem("s_c")
        s_in = sem("s_in")
        s_w = [sem(f"s_w{i}") for i in range(3)]
        s_wm = [sem(f"s_wm{i}") for i in range(6)]
        s_x = [sem(f"s_x{i}") for i in range(4)]
        s_rows = sem("s_rows")
        s_modst = sem("s_modst")
        s_stk = [[sem(f"s_stk{k}{i}") for i in range(2)] for k in range(2)]
        s_st = [sem(f"s_st{i}") for i in range(2)]
        s_id = sem("s_id")
        s_idle = sem("s_idle")
        s_const = sem("s_const")
        s_v = sem("s_v")
        s_wsplit = sem("s_wsplit")
        s_ce = sem("s_ce")
        s_silu = sem("s_silu")
        s_ct = sem("s_ct")
        s_ctc = sem("s_ctc")
        s_mod = sem("s_mod")
        s_modc = sem("s_modc")
        s_modv = sem("s_modv")
        s_mt = sem("s_mt")
        s_zero = sem("s_zero")
        s_halves = sem("s_halves")
        s_sum = sem("s_sum")
        s_bias = sem("s_bias")
        s_table = sem("s_table")
        s_now = sem("s_now")
        s_bn1 = sem("s_bn1")
        s_var1 = sem("s_var1")
        s_r1 = sem("s_r1")
        s_xhat = sem("s_xhat")
        t_pe = sem("t_pe")
        t_evac = sem("t_evac")
        s_hi = sem("s_hi")
        s_ht = sem("s_ht")
        kv_pe = sem("kv_pe")
        kv_evac = sem("kv_evac")
        kv_hi = sem("kv_hi")
        kv_split = sem("kv_split")
        q_pe = sem("q_pe")
        q_evac = sem("q_evac")
        score_pe = sem("score_pe")
        max_done = sem("max_done")
        exp_done = sem("exp_done")
        inv_done = sem("inv_done")
        qn_done = sem("qn_done")
        pv_done = sem("pv_done")
        acc_free = sem("acc_free")
        x2_done = sem("x2_done")
        s_bn2 = sem("s_bn2")
        s_agg1 = sem("s_agg1")
        s_agg2 = sem("s_agg2")
        s_dot = sem("s_dot")
        s_var2 = sem("s_var2")
        s_r2 = sem("s_r2")
        s_xh2 = sem("s_xh2")
        s_hm = sem("s_hm")
        post_done = sem("post_done")

        block = ctx.enter_context(nc.Block())

        wm_stage = [probs[:, j // 2, 2 * (j % 2):2 * (j % 2) + 2, :].rearrange("p a (b n) -> p (a b) n", n=D) for j in range(4)]
        wm_stage += [stacks[1][:, j].bitcast(F32).rearrange("p a n -> p (a n)").rearrange("p (c n) -> p c n", c=CC) for j in range(2)]
        w_stage = [stacks[0][:, j].bitcast(F32).rearrange("p a n -> p (a n)").rearrange("p (c n) -> p c n", c=CC) for j in range(2)]
        w_stage += [hbuf[:].rearrange("p a b n -> p (a b) n")]
        bias_stage = dot_out
        MOD_ORDER = (1, 0, 2, 3, 4, 5)

        UNITS = GB * NQ * HG

        def banks(u):
            return 2 * (u % UNITS) % RING, (2 * (u % UNITS) + 1) % RING

        def wraps(u):
            return banks(u)[1] == 0

        def wrapped(u):
            return sum(wraps(k) for k in range(u))

        def scores_at(u):
            a, z = banks(u)
            return sc[:, a:z + 1, :].rearrange("p a n -> p (a n)")

        def last_user(u, bank):
            return next(d for d in range(1, 4) if bank in banks(u - d))

        WRAPS = wrapped(UNITS)
        @block.sync
        def _(sp):
            for i in range(2):
                sp.sem_inc(s_st[i], 16)
            sp.dma_start(c_sb[:], c).then_inc(s_c, 16)
            sp.dma_start(xt[0][:], x_g[0]).then_inc(s_x[0], 16)

            def stage_mod(j):
                m = MOD_ORDER[j]
                sp.dma_start(wm_stage[j], w_mod[:, m * D:(m + 1) * D].rearrange("(c p) n -> p c n", p=P)).then_inc(s_wm[j], 16)

            stage_mod(0)
            stage_mod(1)
            for k, w in enumerate((Wk, Wv, Wq)):
                sp.dma_start(w_stage[k], w.rearrange("(c p) n -> p c n", p=P)).then_inc(s_w[k], 16)
            for k, b_kv in enumerate((bk, bv)):
                for row in (0, DH):
                    sp.dma_start(bias_stage[row:row + 1, k, :], b_kv.partition_broadcast(1)).then_inc(s_in, 16)
            sp.dma_start(router_row[:], w_router.partition_broadcast(P)).then_inc(s_in, 16)
            with nc.allow_non_contiguous_dma(reason="512 biases and 16 temperatures, once"):
                sp.dma_start(bq_col[:], bq.rearrange("(c p) -> p c", p=P)).then_inc(s_in, 16)
                t_hq = temperature.rearrange("(g q) a b -> q (g a b)", q=HG)
                for hq in range(HG):
                    sp.dma_start(temp_col[DH * hq:DH * (hq + 1), :], t_hq[hq].partition_broadcast(DH)).then_inc(s_in, 16)
            for i in (1, 2):
                sp.dma_start(xt[i][:], x_g[i]).then_inc(s_x[i], 16)
            for j in range(2, 6):
                stage_mod(j)

            def replicate(m_par, k, split_count):
                src, parts = ((k16, (0, 0, 1, 1)), (v16, (0, 1, 0, 1)))[k]
                sp.wait_ge(kv_split, split_count)
                for hq in range(HG):
                    for blk in range(P // DH):
                        sp.dma_start(stacks[m_par][DH * blk:DH * (blk + 1), k, hq, :],
                                     src[DH * hq:DH * (hq + 1), parts[blk], :]).then_inc(s_stk[k][m_par], 16)

            def store_rows(n, par):
                sp.dma_start(h_g[n], hbuf[:, par]).then_inc(s_st[par], 16)
                sp.dma_start(out_g[n], base[:, par]).then_inc(s_st[par], 16)

            sp.wait_ge(s_wsplit, 6)
            replicate(0, 0, 2)
            replicate(0, 1, 4)
            sp.wait_ge(s_modv, 1)
            sp.dma_start(mod_rows, mod_b[:]).then_inc(s_modst, 16)
            sp.wait_ge(s_modst, 16)
            with sp.Fori(0, B) as b:
                ahead = [sp.snap(b * GB + g + 3 if g + 3 < GB else ((b + 1) % B) * GB + (g + 3) % GB) for g in range(GB)]
                before = [sp.snap(b * GB + g - 1 if g >= 1 else ((b + B - 1) % B) * GB + GB - 1) for g in range(GB)]
                for g in range(GB):
                    sp.wait_ge(x2_done, b * GB + g + 1)
                    sp.dma_start(xt[(g + 3) % 4][:], x_g[ahead[g]]).then_inc(s_x[(g + 3) % 4], 16)
                    sp.wait_ge(pv_done, b * GB * NQ + g * NQ + 1)
                    sp.sem_inc(s_idle, 1)
                    replicate((g + 1) % 2, 0, b * GB * 4 + 4 * (g + 1) + 2)
                    replicate((g + 1) % 2, 1, b * GB * 4 + 4 * (g + 1) + 4)
                    sp.wait_ge(post_done, b * GB + g + 1)
                    store_rows(before[g], (g + 1) % 2)
                    if g == 0:
                        for j in range(4):
                            sp.dma_start(rows[:, j, :], mod_rows[b, j].partition_broadcast(P)).then_inc(s_rows, 16)
            sp.wait_ge(post_done, NG + 1)
            store_rows(NG - 1, (NG - 1) % 2)
            for i in range(2):
                sp.wait_ge(s_st[i], 32 * (NG // 2 + i) + 16)
                for k in range(2):
                    sp.wait_ge(s_stk[k][i], 256 * (NG // 2 + 1 - i))
            for i in range(4):
                sp.wait_ge(s_x[i], 16 * (NG // 4 + (i < 3)))

        def stk_count(b, g_next):
            return b * (256 * GB // 2) + 256 * (g_next // 2 + 1)

        @block.tensor
        def _(pe):
            def scores_of(quad_g, i, hq, unit, u):
                par = quad_g % 2
                for half, bank in enumerate(banks(u)):
                    ago = last_user(u, bank)
                    if u >= 0 or unit + 2 > ago:
                        pe.wait_ge(exp_done, unit + 2 - ago)
                    mm = nc.tensor.matmul(sc[:, bank, :],
                                          stacks[par][:, 0, hq, i * P:(i + 1) * P],
                                          stacks[par][:, 1, hq, half * D:(half + 1) * D], start=True, stop=True)
                mm.then_inc(score_pe, 1)

            def kv_slice(par, kk):
                w, p = (wk16, wv16)[kk // 2], kk % 2
                nc.tensor.matmul(pj[:], ones16[:], bias16[:, kk // 2, :], start=True, stop=False)
                terms = [(cc, a, z) for cc in range(CC) for a, z in ((0, 0), (1, 0), (0, 1))]
                for t, (cc, a, z) in enumerate(terms):
                    mm = nc.tensor.matmul(pj[:], hT16[par][:, a, cc, p * P:(p + 1) * P], w[:, z, cc, :],
                                          start=False, stop=(t == len(terms) - 1))
                    if t == 5:
                        yield
                mm.then_inc(kv_pe, 1)

            def q_slice(par, s):
                for ci in range(2):
                    co = 2 * s + ci
                    terms = [(cc, a, z) for cc in range(CC) for a, z in ((0, 0), (1, 0), (0, 1))]
                    for t, (cc, a, z) in enumerate(terms):
                        mm = nc.tensor.matmul(pj[:, ci * 2 * P:(ci + 1) * 2 * P],
                                              wq16[:, z, cc, co * P:(co + 1) * P], hT16[par][:, a, cc, :],
                                              start=(t == 0), stop=(t == len(terms) - 1))
                    if ci == 0:
                        yield
                mm.then_inc(q_pe, 1)

            def t_slice(s):
                for ci in range(2):
                    for p in range(2):
                        mm = nc.tensor.transpose(pj[:, ci * 2 * P + p * P:ci * 2 * P + (p + 1) * P],
                                                 xhat[:, p, (2 * s + ci) * P:(2 * s + ci + 1) * P], ident[:])
                mm.then_inc(t_pe, 1)

            def whole(piece):
                for _ in piece:
                    pass

            def pv_half(g, i, half):
                for hq in range(HG):
                    mm = nc.tensor.matmul(acc[DH * hq:DH * (hq + 1), half * D:(half + 1) * D],
                                          qn[:, i % 2, hq, :], probs[:, i % 2, hq, half * D:(half + 1) * D],
                                          start=(i == 0), stop=(i == NQ - 1))
                if half == 1:
                    mm.then_inc(pv_done, 1)

            pe.sem_inc(pv_done, 1)
            pe.wait_ge(s_id, 2)
            pe.wait_ge(s_silu, 1)
            for cc in range(CC):
                mm = nc.tensor.transpose(pj[:, cc * B:(cc + 1) * B], c_e[:, cc * P:(cc + 1) * P], ident[0:B, 0:B])
            mm.then_inc(s_ct, 1)
            pe.wait_ge(s_ctc, 1)
            mod_banks = [sc[0:B, j, :] for j in range(4)]

            def modulate(j):
                pe.wait_ge(s_wm[j], 16)
                for cc in range(CC):
                    mm = nc.tensor.matmul(mod_banks[j % 4], cT[:, cc, :], wm_stage[j][:, cc, :], start=(cc == 0), stop=(cc == CC - 1))
                mm.then_inc(s_mod, 1)

            modulate(0)
            modulate(1)
            pe.wait_ge(s_mt, 1)
            for k in range(2 * CC):
                src = mod_t[:, k // CC, (k % CC) * P:(k % CC + 1) * P]
                mm = nc.tensor.transpose(sc[:, 4, k * B:(k + 1) * B], src, ident[0:B, 0:B])
            mm.then_inc(s_ct, 1)
            pe.wait_ge(s_xhat, 1)
            t_slice(0)
            pe.wait_ge(t_evac, 1)
            t_slice(1)
            pe.wait_ge(s_ht, 1)
            pe.wait_ge(s_wsplit, 6)
            pe.wait_ge(s_bias, 3)
            for kk in range(4):
                if kk >= 1:
                    pe.wait_ge(kv_evac, kk)
                whole(kv_slice(0, kk))
            pe.wait_ge(kv_evac, 4)
            pe.wait_ge(s_xhat, 2)
            t_slice(0)
            pe.wait_ge(t_evac, 3)
            t_slice(1)
            pe.wait_ge(t_evac, 4)
            whole(q_slice(0, 0))
            pe.wait_ge(q_evac, 1)
            whole(q_slice(0, 1))
            for j in range(2, 6):
                modulate(j)
            for k in range(2):
                pe.wait_ge(s_stk[k][0], 256)
            pe.wait_ge(s_modc, 1)
            for hq in range(HG):
                scores_of(0, 0, hq, hq, hq - HG)

            with pe.Fori(0, B) as b:
                for g in range(GB):
                    n4 = b * (GB * 4) + 4 * (g + 1)
                    n2 = b * (GB * 2) + 2 * (g + 1)
                    for i in range(NQ):
                        nxt = (g + 1) % 2
                        piece = (kv_slice(nxt, i), kv_slice(nxt, i), kv_slice(nxt, i), kv_slice(nxt, i),
                                 None, None, q_slice(nxt, 0), q_slice(nxt, 1))[i]
                        bank_free = ((q_evac, n2), (kv_evac, n4 + 1), (kv_evac, n4 + 2), (kv_evac, n4 + 3),
                                     (kv_evac, n4 + 4), (t_evac, n2 + 3), (t_evac, n2 + 4), (q_evac, n2 + 1))[i]
                        qg, qi = (g, i + 1) if i + 1 < NQ else (g + 1, 0)
                        u = (g * NQ + i) * HG
                        unit = b * UNITS + u + HG
                        if qi == 0:
                            for k in range(2):
                                pe.wait_ge(s_stk[k][qg % 2], stk_count(b, g + 1))
                        scores_of(qg, qi, 0, unit, u)
                        if i == 0:
                            pe.wait_ge(s_ht, b * GB + g + 2)
                        if i == 4:
                            pe.wait_ge(s_xhat, b * GB + g + 3)
                        pe.wait_ge(*bank_free)
                        if piece is None:
                            t_slice(i - 4)
                        else:
                            next(piece)
                        scores_of(qg, qi, 1, unit + 1, u + 1)
                        if piece is not None:
                            whole(piece)
                        scores_of(qg, qi, 2, unit + 2, u + 2)
                        pe.wait_ge(qn_done, b * (GB * NQ) + g * NQ + i + 1)
                        if i == 0:
                            pe.wait_ge(acc_free, b * GB + g + 1)
                        pv_half(g, i, 0)
                        scores_of(qg, qi, 3, unit + 3, u + 3)
                        pv_half(g, i, 1)

        @block.scalar
        def _(act):
            act.wait_ge(s_const, 1)
            nc.scalar.activation(warm[:], warm[:], ACT.Exp).then_inc(exp_done, 1)
            act.wait_ge(s_c, 16)
            nc.scalar.activation(c_e[:], c_sb[:], ACT.Exp, scale=-1.0).then_inc(s_ce, 1)

            def evac_kv(g, kk, count, free):
                act.wait_ge(kv_pe, count)
                if free is not None:
                    act.wait_ge(kv_split, free)
                nc.scalar.activation(kv32[kk % 2][:], pj[:], ACT.Identity,
                                     scale=tempw_col[:, g:g + 1] if kk < 2 else 1.0 / WS).then_inc(kv_evac, 1)

            def evac_t(s, count):
                act.wait_ge(t_pe, count)
                for ci in range(2):
                    cc = 2 * s + ci
                    a = nc.scalar.activation(hT32[:, cc, :], pj[:, ci * 2 * P:(ci + 1) * 2 * P], ACT.Identity,
                                             bias=mod_now[:, CC + cc:CC + cc + 1], scale=mod_now[:, cc:cc + 1])
                a.then_inc(t_evac, 1)

            def evac_q(par, s, count):
                act.wait_ge(q_pe, count)
                for ci in range(2):
                    cc = 2 * s + ci
                    a = nc.scalar.activation(qT[par][:, cc, :], pj[:, ci * 2 * P:(ci + 1) * 2 * P], ACT.Identity,
                                             bias=bq_col[:, cc:cc + 1], scale=1.0 / WS)
                a.then_inc(q_evac, 1)

            def exp_unit(par, hq, count, u):
                act.wait_ge(max_done, count)
                if wraps(u):
                    for half, (bank, total) in enumerate(zip(banks(u), (rsum[:, par, hq:hq + 1], rhalf[:, par:par + 1]))):
                        a = nc.scalar.activation(probs[:, par, hq, half * D:(half + 1) * D], sc[:, bank, :], ACT.Exp,
                                                 bias=nmax[:, par, hq:hq + 1], accum_out=total)
                else:
                    a = nc.scalar.activation(probs[:, par, hq, :], scores_at(u), ACT.Exp,
                                             bias=nmax[:, par, hq:hq + 1], accum_out=rsum[:, par, hq:hq + 1])
                a.then_inc(exp_done, 1)

            act.wait_ge(s_now, 1)
            evac_t(0, 1)
            evac_t(1, 2)
            act.wait_ge(s_in, 10 * 16)
            act.wait_ge(s_bias, 1)
            for kk in range(4):
                evac_kv(0, kk, kk + 1, kk - 1 if kk >= 2 else None)
            act.wait_ge(s_ht, 1)
            evac_t(0, 3)
            evac_t(1, 4)
            evac_q(0, 0, 1)
            evac_q(0, 1, 2)
            for hq in range(HG):
                exp_unit(0, hq, hq + 1, hq - HG)
            with act.Fori(0, B) as b:
                for g in range(GB):
                    n4 = b * (GB * 4) + 4 * (g + 1)
                    n2 = b * (GB * 2) + 2 * (g + 1)
                    for i in range(NQ):
                        act.wait_ge(pv_done, b * (GB * NQ) + g * NQ + i + 1)
                        u = (g * NQ + i) * HG
                        for hq in range(HG):
                            exp_unit((i + 1) % 2, hq, b * UNITS + u + HG + hq + 1, u + hq)
                            if hq != 1:
                                continue
                            if i < 4:
                                evac_kv((g + 1) % GB, i, n4 + i + 1, n4 + i - 1)
                            elif i < 6:
                                if i == 4 and g == 2:
                                    act.wait_ge(t_evac, n2 + 2)
                                    nc.scalar.activation(mod_now[:], mod_table[:, b + 1, :], ACT.Identity).then_inc(s_now, 1)
                                if i == 4:
                                    act.wait_ge(s_ht, b * GB + g + 2)
                                    act.wait_ge(s_now, b + 1 + (g >= 2))
                                evac_t(i - 4, n2 + i - 1)
                            else:
                                evac_q((g + 1) % 2, i - 6, n2 + i - 5)

        @block.vector
        def _(dve):
            nc.vector.memset(acc[:], 0.0)
            nc.vector.memset(warm[:], 0.0).then_inc(s_const, 1)
            nc.vector.memset(minus_half[:], -0.5).then_inc(s_const, 1)
            dve.wait_ge(s_ce, 1)
            nc.vector.tensor_scalar(mod_t[:, 0, :], c_e[:], 1.0, None, ALU.add).then_inc(s_v, 1)
            dve.wait_ge(s_v, 1)
            nc.vector.reciprocal(mod_t[:, 1, :], mod_t[:, 0, :]).then_inc(s_v, 1)
            dve.wait_ge(s_v, 2)
            nc.vector.tensor_tensor(c_e[:], c_sb[:], mod_t[:, 1, :], ALU.mult).then_inc(s_silu, 1)
            dve.wait_ge(s_ct, 1)
            nc.vector.tensor_copy(cT[:], pj[:, 0:CC * B].rearrange("p (c b) -> p c b", b=B)).then_inc(s_ctc, 1)

            def wait_alone(s, count):
                dve.wait_ge(s, count)
                dve.sem_inc(s_idle, 1)

            def stats_of_x(buf, loads, count):
                dve.wait_ge(s_x[buf], loads)
                for p in range(2):
                    st = nc.vector.bn_stats(stats1[:, p, :], xt[buf][:, p, :])
                st.then_inc(s_bn1, 1)

            def aggregate(count):
                wait_alone(s_bn1, count)
                for p in range(2):
                    st = nc.vector.bn_aggr(mv1[:, p, :], stats1[:, p, :])
                st.then_inc(s_agg1, 1)
                dve.wait_ge(s_agg1, count)
                nc.vector.tensor_scalar(var1[:], mv1[:, :, 1], EPS, None, ALU.add)
                nc.vector.tensor_scalar(nmean1[:], mv1[:, :, 0], -1.0, None, ALU.mult).then_inc(s_var1, 1)

            stats_of_x(0, 16, 1)
            aggregate(1)
            mod_banks = [sc[0:B, j, :] for j in range(4)]
            dve.wait_ge(s_mod, 1)
            nc.vector.tensor_scalar(mod_t[:, 0, :], mod_banks[0], 1.0, None, ALU.add)
            dve.wait_ge(s_mod, 2)
            nc.vector.tensor_copy(mod_t[:, 1, :], mod_banks[1]).then_inc(s_mt, 1)
            dve.wait_ge(s_ct, 2)
            tab = sc[:, 4, 0:2 * CC * B].rearrange("p (k b) -> p b k", b=B)
            nc.vector.tensor_copy(mod_table[:, B, :], tab[:, B - 1, :])
            nc.vector.tensor_copy(mod_now[:], tab[:, 0, :]).then_inc(s_now, 1)
            nc.vector.tensor_copy(mod_table[:, 0:B, :], tab).then_inc(s_table, 1)
            for k, (w16, st) in enumerate(zip((wk16, wv16, wq16), w_stage)):
                dve.wait_ge(s_w[k], 16)
                nc.vector.tensor_scalar(w16[:, 0], st, WS, None, ALU.mult).then_inc(s_wsplit, 1)
                dve.wait_ge(s_wsplit, 2 * k + 1)
                nc.vector.scalar_tensor_tensor(out=w16[:, 1], in0=st, scalar=WS, in1=w16[:, 0],
                                               op0=ALU.mult, op1=ALU.subtract).then_inc(s_wsplit, 1)
            dve.wait_ge(s_in, 10 * 16)
            nc.vector.tensor_scalar(tempw_col[:], temp_col[:], 1.0 / WS, None, ALU.mult).then_inc(s_bias, 1)
            dve.wait_ge(s_bias, 2)
            lo_row = slice(DH, DH + 1)
            nc.vector.tensor_scalar(bias16[0:1], bias_stage[0:1], WS, None, ALU.mult)
            nc.vector.tensor_scalar(bias16[lo_row], bias_stage[lo_row], WS, None, ALU.mult).then_inc(s_v, 1)
            dve.wait_ge(s_v, 3)
            nc.vector.scalar_tensor_tensor(out=bias16[lo_row], in0=bias_stage[lo_row], scalar=WS, in1=bias16[lo_row],
                                           op0=ALU.mult, op1=ALU.subtract).then_inc(s_bias, 1)

            def row_max(par, hq, count, b, u):
                dve.wait_ge(score_pe, count)
                dst = nmax[:, par, hq:hq + 1]
                if wraps(u):
                    for half, bank in enumerate(banks(u)):
                        r = nc.vector.tensor_reduce(nhalf[:, half:half + 1], sc[:, bank, :], AX.X, ALU.max, negate=True)
                    r.then_inc(s_halves, 1)
                    dve.wait_ge(s_halves, 1 if u < 0 else b * WRAPS + (wrapped(u) + 2))
                    nc.vector.tensor_tensor(dst, nhalf[:, 0:1], nhalf[:, 1:2], ALU.min).then_inc(max_done, 1)
                else:
                    nc.vector.tensor_reduce(dst, scores_at(u), AX.X, ALU.max, negate=True).then_inc(max_done, 1)

            dve.wait_ge(s_xhat, 1)
            stats_of_x(1, 16, 2)
            aggregate(2)
            for k, (row, add) in enumerate(((0, 0.0), (2, 0.0), (1, 1.0), (3, 0.0))):
                dve.wait_ge(s_mod, k + 3)
                last = nc.vector.tensor_scalar(mod_b[:, row, :], mod_banks[(k + 2) % 4], add, None, ALU.add)
            last.then_inc(s_modc, 1)
            dve.wait_ge(s_modc, 1)
            v = 3
            for row in (0, 3):
                gate = mod_b[:, row, :]
                nc.vector.tensor_scalar(sign, gate, 0.0, 2.0, ALU.is_ge, ALU.mult).then_inc(s_v, 1)
                nc.vector.scalar_tensor_tensor(out=size, in0=gate, scalar=-1.0, in1=gate, op0=ALU.mult, op1=ALU.max).then_inc(s_v, 1)
                dve.wait_ge(s_v, v + 2)
                nc.vector.tensor_scalar(sign, sign, -1.0, None, ALU.add).then_inc(s_v, 1)
                dve.wait_ge(s_v, v + 3)
                nc.vector.scalar_tensor_tensor(out=gate, in0=size, scalar=GATE_MIN, in1=sign,
                                               op0=ALU.max, op1=ALU.mult).then_inc(s_v, 1)
                dve.wait_ge(s_v, v + 4)
                v += 4
            nc.vector.tensor_copy(size, sign).then_inc(s_modv, 1)
            for hq in range(HG):
                row_max(0, hq, hq + 1, 0, hq - HG)

            def dot_router(p, b, g):
                nc.vector.scalar_tensor_tensor(out=dot_out[:, p], in0=hbuf[:, (g + 1) % 2, p, :], scalar=1.0, in1=router_row[:],
                                               op0=ALU.mult, op1=ALU.mult,
                                               accum_out=scores[:, bass.ds(b * (2 * GB) + 2 * g + p, 1)]).then_inc(s_dot, 1)

            def gated(b, g):
                dve.wait_ge(pv_done, b * (GB * NQ) + g * NQ + 1)
                if g == 1:
                    dve.wait_ge(s_rows, b * 64 + 64)
                nc.vector.tensor_tensor(x2[:], acc[:].rearrange("q (p n) -> q p n", p=2),
                                        rows[:, 0:1, :].broadcast_to([P, 2, D]), ALU.mult).then_inc(acc_free, 1)

            def stats_of_x2(b, g):
                dve.wait_ge(x2_done, b * GB + g + 1)
                for p in range(2):
                    st = nc.vector.bn_stats(stats2[:, p, :], x2[:, p, :])
                st.then_inc(s_bn2, 1)

            def aggregate2(b, g):
                wait_alone(s_bn2, b * GB + g + 1)
                for p in range(2):
                    st = nc.vector.bn_aggr(mv2[:, p, :], stats2[:, p, :])
                st.then_inc(s_agg2, 1)
                dve.wait_ge(s_agg2, b * GB + g + 1)
                nc.vector.tensor_scalar(var2[:], mv2[:, :, 1], EPS, None, ALU.add)
                nc.vector.tensor_scalar(nmean2[:], mv2[:, :, 0], -1.0, None, ALU.mult).then_inc(s_var2, 1)

            def q_over_sums(b, g, i):
                u = (g * NQ + i) * HG
                dve.wait_ge(exp_done, b * UNITS + u + HG + 1)
                for hq in range(HG):
                    if wraps(u - HG + hq):
                        total = rsum[:, i % 2, hq:hq + 1]
                        nc.vector.tensor_tensor(total, total, rhalf[:, i % 2:i % 2 + 1], ALU.add).then_inc(s_sum, 1)
                        dve.wait_ge(s_sum, b * WRAPS + (wrapped(u) + 1))
                nc.vector.reciprocal(rinv[:, i % 2, :], rsum[:, i % 2, :]).then_inc(inv_done, 1)
                if i == 0:
                    dve.wait_ge(q_evac, b * (2 * GB) + 2 * (g + 1))
                dve.wait_ge(inv_done, b * (GB * NQ) + g * NQ + i + 1)
                nc.vector.tensor_tensor(
                    qn[:, i % 2], qT[g % 2][:, i % CC, (i // CC) * P:(i // CC + 1) * P].rearrange("p (h j) -> p h j", j=DH),
                    rinv[:, i % 2, :].unsqueeze(2).broadcast_to([P, HG, DH]), ALU.mult).then_inc(qn_done, 1)

            with dve.Fori(0, B) as b:
                for g in range(GB):
                    for i in range(NQ):
                        par = (i + 1) % 2
                        u = (g * NQ + i) * HG
                        unit = b * UNITS + u + HG
                        for hq in range(HG):
                            row_max(par, hq, unit + hq + 1, b, u + hq)
                            if hq == 0 and i == 0:
                                gated(b, g)
                            if hq == QN_AFTER:
                                q_over_sums(b, g, i)
                            if hq == 1 and i == 1:
                                dve.wait_ge(s_xhat, b * GB + g + 2)
                                stats_of_x((g + 2) % 4, b * 16 + 16 * ((g + 2) // 4 + 1), b * GB + g + 3)
                            if hq == 2 and i == 1:
                                aggregate(b * GB + g + 3)
                            if hq == 1 and i == 2:
                                stats_of_x2(b, g)
                            if hq == 2 and i == 2:
                                aggregate2(b, g)
                            if hq == 1 and i >= 6:
                                dve.wait_ge(post_done, b * GB + g + 1)
                                dot_router(i - 6, b, g)
            gated(B, 0)
            stats_of_x2(B, 0)
            aggregate2(B, 0)
            dve.wait_ge(post_done, NG + 1)
            for p in range(2):
                dot_router(p, B, 0)
            dve.wait_ge(s_dot, 2 * NG + 2)

        @block.gpsimd
        def _(pool):
            nc.gpsimd.memset(ident[:], 0.0).then_inc(s_id, 1)
            pool.wait_ge(s_id, 1)
            nc.gpsimd.affine_select(out=ident[:], in_=ident[:], compare_op=ALU.not_equal, fill=1.0, base=0,
                                    pattern=[[-1, P]], channel_multiplier=1).then_inc(s_id, 1)
            pool.wait_ge(s_const, 2)
            nc.gpsimd.memset(ones16[:], 1.0)
            nc.gpsimd.memset(bias16[:], 0.0).then_inc(s_bias, 1)
            nc.gpsimd.memset(rows[:], 0.0)
            nc.gpsimd.memset(xt[3][:], 0.0).then_inc(s_zero, 1)

            def wait_alone(s, count):
                pool.wait_ge(s, count)
                pool.sem_inc(s_idle, 1)

            def normed(dst, src, var, nmean, rstd, s_var, s_r, s_out, count):
                pool.wait_ge(s_var, count)
                nc.gpsimd.tensor_tensor(rstd[:], var[:], minus_half[:], ALU.pow).then_inc(s_r, 1)
                wait_alone(s_r, count)
                for p in range(2):
                    last = nc.gpsimd.tensor_scalar(dst[:, p, :], src[:, p, :], nmean[:, p:p + 1], rstd[:, p:p + 1], ALU.add, ALU.mult)
                last.then_inc(s_out, 1)

            def split_hT(par, count, t_count):
                wait_alone(t_evac, t_count)
                nc.gpsimd.tensor_scalar(hT16[par][:, 0], hT32[:], 1.0, None, ALU.mult).then_inc(s_hi, 1)
                pool.wait_ge(s_hi, count)
                nc.gpsimd.tensor_tensor(hT16[par][:, 1], hT32[:], hT16[par][:, 0], ALU.subtract).then_inc(s_ht, 1)

            def split_kv(kk, count):
                dst = (k16, v16)[kk // 2][:, :, (kk % 2) * D:(kk % 2 + 1) * D]
                wait_alone(kv_evac, count)
                nc.gpsimd.tensor_scalar(dst[:, 0], kv32[kk % 2][:], 1.0, None, ALU.mult).then_inc(kv_hi, 1)
                pool.wait_ge(kv_hi, count)
                nc.gpsimd.tensor_tensor(dst[:, 1], kv32[kk % 2][:], dst[:, 0], ALU.subtract).then_inc(kv_split, 1)

            normed(xhat, xt[0], var1, nmean1, rstd1, s_var1, s_r1, s_xhat, 1)
            split_hT(0, 1, 2)
            pool.wait_ge(t_pe, 2)
            pool.wait_ge(s_wsplit, 6)
            normed(xhat, xt[1], var1, nmean1, rstd1, s_var1, s_r1, s_xhat, 2)
            for kk in range(4):
                split_kv(kk, kk + 1)
            split_hT(1, 2, 4)

            def residual(b, g):
                pool.wait_ge(acc_free, b * GB + g + 1)
                nc.gpsimd.tensor_tensor(x2[:], x2[:], xt[(g + 3) % 4][:], ALU.add).then_inc(x2_done, 1)

            def post(b, g):
                n = b * GB + g + 1
                par = (g + 1) % 2
                pool.wait_ge(s_st[par], b * (32 * GB // 2) + 32 * (g // 2) + 16)
                h, bs = hbuf[:, par], base[:, par]
                normed(h, x2, var2, nmean2, rstd2, s_var2, s_r2, s_xh2, n)
                steps = ((h, h, 1, ALU.mult), (h, h, 2, ALU.add), (bs, h, 3, ALU.mult))
                pool.wait_ge(s_xh2, n)
                for k, (dst, a, row, op) in enumerate(steps):
                    nc.gpsimd.tensor_tensor(dst, a, rows[:, row:row + 1, :].broadcast_to([P, 2, D]), op).then_inc(s_hm, 1)
                    pool.wait_ge(s_hm, b * (3 * GB) + 3 * g + k + 1)
                nc.gpsimd.tensor_tensor(bs, bs, x2[:], ALU.add).then_inc(post_done, 1)

            with pool.Fori(0, B) as b:
                for g in range(GB):
                    n4 = b * (GB * 4) + 4 * (g + 1)
                    n3 = b * GB + g + 3
                    residual(b, g)
                    split_kv(0, n4 + 1)
                    split_kv(1, n4 + 2)
                    pool.wait_ge(t_pe, b * (2 * GB) + 2 * (g + 2))
                    normed(xhat, xt[(g + 2) % 4], var1, nmean1, rstd1, s_var1, s_r1, s_xhat, n3)
                    split_kv(2, n4 + 3)
                    split_kv(3, n4 + 4)
                    post(b, g)
                    split_hT(g % 2, n3, b * (2 * GB) + 2 * (g + 3))
            residual(B, 0)
            post(B, 0)


def ffn_phase(nc, W1, b1, W2, b2, out, h_rows, sel_rows, mod_rows, scores):
    out_rows = out.rearrange("b t d -> (b t) d")
    sel_b = sel_rows.rearrange("(b k s) w -> b s k w", b=B, s=P)
    TB = 2 * GB
    KT = KEEP // P
    PAD = (GB - 1) * 2 * P

    with ExitStack() as ctx:
        def sb(name, shape, dt):
            return ctx.enter_context(nc.sbuf_tensor(name, shape, dt))

        def pb(name, shape):
            return ctx.enter_context(nc.psum_tensor(name, shape, F32))

        def sem(name):
            return ctx.enter_context(nc.semaphore(name))

        w1_16 = sb("w1_16", [P, 2, CC, F], F16)
        w2_16 = sb("w2_16", [P, 2, FC, D], F16)
        stage = sb("stage", [P, 4, 4, D], F32)
        b1_col = sb("b1_col", [P, FC], F32)
        b2_row = sb("b2_row", [P, D], F32)
        gb_row = sb("gb_row", [P, 2, D], F32)
        id2 = sb("id2", [P, P], F32)
        ones = sb("ones", [P, P], F32)
        earlier = sb("earlier", [P, 2, PAD + 2 * P + PAD], BF16)
        tok_i = sb("tok_i", [P, B * TB], I32)
        e_neg = sb("e_neg", [P, B * TB], F32)
        tokens = sb("tokens", [P, B * TB, 2], F32)
        warm2 = sb("warm2", [P, 1], F32)
        s8 = sb("s8", [P, TB], F32)
        diag = sb("diag", [P, TB, P], F32)
        srow = sb("srow", [P, TB, P], F32)
        scol = sb("scol", [P, TB], F32)
        cmp_out = sb("cmp_out", [P, 2, TB * P], BF16)
        above = sb("above", [P, TB], F32)
        ties = sb("ties", [P, TB], F32)
        rank = sb("rank", [P, TB], F32)
        drop = sb("drop", [P, TB], F32)
        first = sb("first", [P, 1], F32)
        slot = sb("slot", [P, TB], I32)
        tok8 = sb("tok8", [P, TB, 2], F32)
        kept = sb("kept", [P, 2, KT, 2], F32)
        kept_i = sb("kept_i", [P, 2, KT], I32)
        hs = sb("hs", [P, 2, KT, D], F32)
        bs = sb("bs", [P, 2, KT, D], F32)
        fT16 = sb("fT16", [P, 2, 2, CC, KEEP], F16)
        g32 = sb("g32", [P, 2, KEEP], F32)
        g16 = sb("g16", [P, 2, 2, KEEP], F16)
        y = sb("y", [P, 2, KT, D], F32)

        acc = [pb(f"ff2_{k}", [P, D]) for k in range(KT)]
        ff = [pb(f"ff1_{k}", [P, KEEP]) for k in range(2)]
        aux = [pb(f"aux{k}", [P, D]) for k in range(2)]

        s_stage = [sem(f"s_stage{i}") for i in range(8)]
        s_b = sem("s_b")
        s_gb = [sem(f"s_gb{i}") for i in range(2)]
        w_hi = sem("w_hi")
        w_lo = sem("w_lo")
        s_idle = sem("s_idle2")
        s_c2 = sem("s_c2")
        s_e = sem("s_e")
        s_d = sem("s_d")
        s_s8 = sem("s_s8")
        s_diag = sem("s_diag")
        s_bc = sem("s_bc")
        s_srow = sem("s_srow")
        s_ext = sem("s_ext")
        s_cmp = sem("s_cmp")
        s_rank = sem("s_rank")
        s_slot = sem("s_slot")
        s_sel = sem("s_sel")
        s_kept = [sem(f"s_kept{i}") for i in range(2)]
        s_ids = sem("s_ids")
        s_gh = [sem(f"s_gh{i}") for i in range(2)]
        s_gbs = [sem(f"s_gbs{i}") for i in range(2)]
        ft_pe = sem("ft_pe")
        ft_hi = sem("ft_hi")
        ft_lo = sem("ft_lo")
        ff1_pe = sem("ff1_pe")
        gelu_done = sem("gelu_done")
        g_hi = sem("g_hi")
        g_split = sem("g_split")
        ff2_pe = sem("ff2_pe")
        acc_out = sem("acc_out")
        y_gb = sem("y_gb")
        y_done = sem("y_done")
        s_out = [sem(f"s_out{i}") for i in range(2)]

        block = ctx.enter_context(nc.Block())

        def batches(eng, body):
            with eng.Fori(0, B // 2 - 1) as bb:
                for par in range(2):
                    body(bb, par, False)
            for par in range(2):
                body(B // 2 - 1, par, par == 1)

        def n_of(bb, par, per, off):
            return bb * (2 * per) + (per * par + off)

        @block.sync
        def _(sp):
            def load_kept(bb, par):
                with nc.allow_non_contiguous_dma(reason="number and weight of 512 tokens"):
                    sp.wait_ge(s_sel, n_of(bb, par, 16 * TB, 16 * TB))
                    sp.dma_start(kept[:, par], sel_b[bb * 2 + par]).then_inc(s_kept[par], 16)

            for j in range(8):
                if j == 7:
                    load_kept(0, 0)
                if j < 4:
                    src = W1[:, j * D:(j + 1) * D].rearrange("(c p) n -> p c n", p=P)
                else:
                    src = W2[(j - 4) * 4 * P:(j - 3) * 4 * P, :].rearrange("(k p) n -> p k n", p=P)
                    sp.wait_ge(w_lo, j - 3)
                sp.dma_start(stage[:, j % 4], src).then_inc(s_stage[j], 16)
                if j == 3:
                    sp.dma_start(b2_row[:], b2.partition_broadcast(P)).then_inc(s_b, 16)
                    with nc.allow_non_contiguous_dma(reason="2048 biases, once"):
                        sp.dma_start(b1_col[:], b1.rearrange("(f p) -> p f", p=P)).then_inc(s_b, 16)

            def body(bb, par, last):
                sp.wait_ge(y_done, n_of(bb, par, KT, 0) + 1)
                sp.dma_start(gb_row[:, par], mod_rows[bb * 2 + par, 3].partition_broadcast(P)).then_inc(s_gb[par], 16)
                if not last:
                    load_kept(bb + (par == 1), 1 - par)

            batches(sp, body)
            for i in range(2):
                sp.wait_ge(s_out[i], 16 * KT * B // 2)

        @block.tensor
        def _(pe):
            def broadcast_scores(bb, par):
                pe.wait_ge(s_diag, n_of(bb, par, 1, 1))
                for k in range(2):
                    mm = nc.tensor.matmul(aux[k][:], ones[:], diag[:, k * TB // 2:(k + 1) * TB // 2, :], start=True, stop=True)
                mm.then_inc(s_bc, 1)

            def transpose_kept(bb, par, cc):
                if cc == 0:
                    pe.wait_ge(s_gh[par], bb * (16 * KT) + 16 * KT)
                    pe.wait_ge(s_srow, n_of(bb, par, 1, 1))
                if cc >= 2:
                    pe.wait_ge(ft_lo, n_of(bb, par, CC, cc - 1))
                for kt in range(KT):
                    mm = nc.tensor.transpose(aux[cc % 2][:, kt * P:(kt + 1) * P], hs[:, par, kt, cc * P:(cc + 1) * P], id2[:])
                mm.then_inc(ft_pe, 1)

            def ff1(bb, par, f):
                pe.wait_ge(gelu_done, n_of(bb, par, FC, f + 1))
                if f % 4 == 0:
                    pe.wait_ge(w_lo, f // 4 + 1)
                terms = [(cc, a, z) for cc in range(CC) for z, a in ((0, 0), (0, 1), (1, 0))]
                for t, (cc, a, z) in enumerate(terms):
                    mm = nc.tensor.matmul(ff[f % 2][:], w1_16[:, z, cc, f * P:(f + 1) * P], fT16[:, par, a, cc, :],
                                          start=(t == 0), stop=(t == len(terms) - 1))
                mm.then_inc(ff1_pe, 1)

            def ff2(bb, par, f):
                if f % 4 == 0:
                    pe.wait_ge(w_lo, 4 + f // 4 + 1)
                if f == 0:
                    pe.wait_ge(acc_out, n_of(bb, par, KT, 0) + 1)
                pe.wait_ge(g_split, n_of(bb, par, FC, f + 3))
                for kt in range(KT):
                    for t, (a, z) in enumerate(((0, 0), (0, 1), (1, 0))):
                        mm = nc.tensor.matmul(acc[kt][:], g16[:, f % 2, a, kt * P:(kt + 1) * P], w2_16[:, z, f, :],
                                              start=(f == 0 and t == 0), stop=(f == FC - 1 and t == 2))
                mm.then_inc(ff2_pe, 1)

            pe.wait_ge(s_c2, 3)
            broadcast_scores(0, 0)
            for cc in range(CC):
                transpose_kept(0, 0, cc)

            def body(bb, par, last):
                pe.wait_ge(ft_lo, n_of(bb, par, CC, CC))
                for f in range(FC):
                    ff1(bb, par, f)
                    if f >= 1:
                        ff2(bb, par, f - 1)
                    if not last and f == 1:
                        broadcast_scores(bb + (par == 1), 1 - par)
                    if not last and f >= FC - CC:
                        transpose_kept(bb + (par == 1), 1 - par, f - (FC - CC))
                ff2(bb, par, FC - 1)

            batches(pe, body)

        @block.scalar
        def _(act):
            nc.scalar.activation(e_neg[:], scores[:, 2:], ACT.Exp, scale=-1.0).then_inc(s_e, 1)

            def high_part(j):
                act.wait_ge(s_stage[j], 16)
                if j < 4:
                    dst = w1_16[:, 0, :, j * D:(j + 1) * D]
                else:
                    dst = w2_16[:, 0, 4 * (j - 4):4 * (j - 3), :]
                nc.scalar.activation(dst, stage[:, j % 4], ACT.Identity, scale=WS).then_inc(w_hi, 1)

            def copy_scores(bb, par):
                act.wait_ge(s_bc, n_of(bb, par, 1, 1))
                for k in range(2):
                    a = nc.scalar.activation(srow[:, k * TB // 2:(k + 1) * TB // 2, :].rearrange("p a b -> p (a b)"), aux[k][:], ACT.Identity)
                a.then_inc(s_srow, 1)

            def kept_high(bb, par, cc):
                act.wait_ge(ft_pe, n_of(bb, par, CC, cc + 1))
                nc.scalar.activation(fT16[:, par, 0, cc, :], aux[cc % 2][:], ACT.Identity).then_inc(ft_hi, 1)

            for j in range(2):
                high_part(j)
            copy_scores(0, 0)
            for j in range(2, 8):
                high_part(j)
            act.wait_ge(s_d, 1)
            nc.scalar.activation(warm2[:], warm2[:], ACT.Gelu_apprx_tanh).then_inc(gelu_done, 2)
            for cc in range(CC):
                kept_high(0, 0, cc)
            act.wait_ge(s_b, 32)

            def body(bb, par, last):
                for f in range(FC):
                    act.wait_ge(g_split, n_of(bb, par, FC, f + 1))
                    act.wait_ge(ff1_pe, n_of(bb, par, FC, f + 1))
                    nc.scalar.activation(g32[:, f % 2, :], ff[f % 2][:], ACT.Gelu_apprx_tanh, bias=b1_col[:, f:f + 1],
                                         scale=1.0 / WS).then_inc(gelu_done, 1)
                    if not last and f == 2:
                        copy_scores(bb + (par == 1), 1 - par)
                    if not last and f > FC - CC:
                        kept_high(bb + (par == 1), 1 - par, f - (FC - CC) - 1)
                if not last:
                    kept_high(bb + (par == 1), 1 - par, CC - 1)

            batches(act, body)

        @block.vector
        def _(dve):
            dve.sem_inc(acc_out, 1)
            dve.sem_inc(y_done, 1)
            nc.vector.memset(warm2[:], 0.0).then_inc(s_d, 1)
            nc.vector.memset(first[:], 0.0)
            nc.vector.memset(g16[:, 0, 0, 0:2], 0.0).then_inc(g_split, 2)
            dve.wait_ge(s_c2, 3)

            def low_part(j):
                dve.wait_ge(w_hi, j + 1)
                if j < 4:
                    hi, lo = (w1_16[:, z, :, j * D:(j + 1) * D] for z in range(2))
                else:
                    hi, lo = (w2_16[:, z, 4 * (j - 4):4 * (j - 3), :] for z in range(2))
                nc.vector.scalar_tensor_tensor(out=lo, in0=stage[:, j % 4], scalar=WS, in1=hi, op0=ALU.mult,
                                               op1=ALU.subtract).then_inc(w_lo, 1)

            def diagonals(bb, par):
                nc.vector.tensor_copy(s8[:], scores[:, bass.ds(bb * (2 * TB) + par * TB + 2, TB)]).then_inc(s_s8, 1)
                dve.wait_ge(s_s8, n_of(bb, par, 1, 1))
                nc.vector.tensor_tensor(diag[:], id2[:].unsqueeze(1).broadcast_to([P, TB, P]),
                                        s8[:].unsqueeze(2).broadcast_to([P, TB, P]), ALU.mult).then_inc(s_diag, 1)

            def own_scores(bb, par):
                dve.wait_ge(s_srow, n_of(bb, par, 1, 1))
                nc.vector.tensor_tensor(diag[:], srow[:], id2[:].unsqueeze(1).broadcast_to([P, TB, P]), ALU.mult).then_inc(s_ext, 1)
                dve.wait_ge(s_ext, n_of(bb, par, 2, 1))
                nc.vector.tensor_reduce(scol[:], diag[:], AX.X, ALU.add).then_inc(s_ext, 1)
                dve.wait_ge(s_ext, n_of(bb, par, 2, 2))

            def count_above(bb, par, t):
                flat = srow[:].rearrange("p a b -> p (a b)")
                if t >= 1:
                    dve.wait_ge(s_cmp, n_of(bb, par, 2 * TB, 2 * t - 1))
                nc.vector.tensor_scalar(cmp_out[:, 0], flat, scol[:, t:t + 1], 0.0, ALU.is_gt, ALU.add,
                                        accum_out=above[:, t:t + 1]).then_inc(s_cmp, 1)
                if t >= 1:
                    dve.wait_ge(s_cmp, n_of(bb, par, 2 * TB, 2 * t))
                at = PAD - (t // 2) * 2 * P
                nc.vector.scalar_tensor_tensor(out=cmp_out[:, 1], in0=flat, scalar=scol[:, t:t + 1],
                                               in1=earlier[:, t % 2, at:at + TB * P], op0=ALU.is_equal, op1=ALU.mult,
                                               accum_out=ties[:, t:t + 1]).then_inc(s_cmp, 1)

            def slots(bb, par):
                dve.wait_ge(s_cmp, n_of(bb, par, 2 * TB, 2 * TB))
                nc.vector.tensor_tensor(rank[:], above[:], ties[:], ALU.add).then_inc(s_rank, 1)
                dve.wait_ge(s_rank, n_of(bb, par, 3, 1))
                nc.vector.tensor_scalar(drop[:], rank[:], float(KEEP), BIG, ALU.is_ge, ALU.mult).then_inc(s_rank, 1)
                dve.wait_ge(s_rank, n_of(bb, par, 3, 2))
                nc.vector.tensor_copy(tok8[:], tokens[:, bass.ds(bb * (2 * TB) + par * TB, TB), :])
                nc.vector.scalar_tensor_tensor(out=slot[:], in0=rank[:], scalar=first[:, 0:1], in1=drop[:],
                                               op0=ALU.add, op1=ALU.add).then_inc(s_slot, 1)
                nc.vector.tensor_scalar(first[:], first[:], float(KEEP), None, ALU.add).then_inc(s_rank, 1)
                dve.wait_ge(s_rank, n_of(bb, par, 3, 3))

            def numbers(bb, par):
                dve.wait_ge(s_kept[par], bb * 16 + 16)
                nc.vector.tensor_copy(kept_i[:, par], kept[:, par, :, 0]).then_inc(s_ids, 1)

            def kept_low(bb, par, cc):
                dve.wait_ge(ft_hi, n_of(bb, par, CC, cc + 1))
                nc.vector.tensor_tensor(fT16[:, par, 1, cc, :], aux[cc % 2][:], fT16[:, par, 0, cc, :], ALU.subtract).then_inc(ft_lo, 1)

            dve.wait_ge(s_e, 1)
            nc.vector.tensor_scalar(e_neg[:], e_neg[:], 1.0, None, ALU.add).then_inc(s_d, 1)
            dve.wait_ge(s_d, 2)
            nc.vector.reciprocal(tokens[:, :, 1], e_neg[:]).then_inc(s_d, 1)
            nc.vector.tensor_copy(tokens[:, :, 0], tok_i[:]).then_inc(s_d, 1)
            dve.wait_ge(s_d, 4)
            diagonals(0, 0)
            low_part(0)
            own_scores(0, 0)
            for t in range(TB):
                count_above(0, 0, t)
            slots(0, 0)
            low_part(1)
            low_part(2)
            numbers(0, 0)
            for j in range(3, 8):
                low_part(j)
            for cc in range(CC):
                kept_low(0, 0, cc)

            def body(bb, par, last):
                nb, npar = bb + (par == 1), 1 - par
                for f in range(FC):
                    dve.wait_ge(gelu_done, n_of(bb, par, FC, f + 3))
                    nc.vector.tensor_copy(g16[:, f % 2, 0, :], g32[:, f % 2, :]).then_inc(g_hi, 1)
                    dve.wait_ge(g_hi, n_of(bb, par, FC, f + 1))
                    nc.vector.tensor_tensor(g16[:, f % 2, 1, :], g32[:, f % 2, :], g16[:, f % 2, 0, :], ALU.subtract).then_inc(g_split, 1)
                    if last:
                        continue
                    if f == 0:
                        diagonals(nb, npar)
                    if f == 3:
                        own_scores(nb, npar)
                    if 4 <= f < 8:
                        count_above(nb, npar, 2 * (f - 4))
                        count_above(nb, npar, 2 * (f - 4) + 1)
                    if f == 7:
                        slots(nb, npar)
                    if f == 10:
                        numbers(nb, npar)
                    if f > FC - CC:
                        kept_low(nb, npar, f - (FC - CC) - 1)
                dve.wait_ge(ff2_pe, n_of(bb, par, FC, FC))
                dve.wait_ge(s_b, 32)
                for kt in range(KT):
                    nc.vector.scalar_tensor_tensor(out=y[:, par, kt, :], in0=acc[kt][:], scalar=1.0 / WS, in1=b2_row[:],
                                                   op0=ALU.mult, op1=ALU.add).then_inc(acc_out, 1)
                if not last:
                    kept_low(nb, npar, CC - 1)
                for kt in range(KT):
                    if kt == 0:
                        dve.wait_ge(s_gbs[par], bb * (16 * KT) + 16 * KT)
                    dve.wait_ge(y_gb, n_of(bb, par, KT, kt + 1))
                    nc.vector.scalar_tensor_tensor(out=y[:, par, kt, :], in0=y[:, par, kt, :], scalar=kept[:, par, kt, 1:2],
                                                   in1=bs[:, par, kt, :], op0=ALU.mult, op1=ALU.add).then_inc(y_done, 1)

            batches(dve, body)

        @block.gpsimd
        def _(pool):
            nc.gpsimd.memset(id2[:], 0.0).then_inc(s_c2, 1)
            nc.gpsimd.memset(ones[:], 1.0)
            for p in range(2):
                nc.gpsimd.memset(earlier[:, p, 0:PAD + 2 * P], 1.0)
                last_one = nc.gpsimd.memset(earlier[:, p, PAD + 2 * P:], 0.0)
            nc.gpsimd.iota(tok_i[:], pattern=[[2 * P, NG], [1, 2]], base=0, channel_multiplier=2).then_inc(s_c2, 1)
            pool.wait_ge(s_c2, 2)
            for p in range(2):
                for pp in range(2):
                    part = earlier[:, p, PAD + pp * P:PAD + (pp + 1) * P]
                    nc.gpsimd.affine_select(out=part, in_=part, compare_op=ALU.is_ge if p > pp else ALU.is_gt, fill=0.0, base=0,
                                            pattern=[[-1, P]], channel_multiplier=1)
            nc.gpsimd.affine_select(out=id2[:], in_=id2[:], compare_op=ALU.not_equal, fill=1.0, base=0,
                                    pattern=[[-1, P]], channel_multiplier=1).then_inc(s_c2, 1)

            def wait_alone(s, count):
                pool.wait_ge(s, count)
                pool.sem_inc(s_idle, 1)

            def store_kept(bb, par):
                wait_alone(s_slot, n_of(bb, par, 1, 1))
                for t in range(TB):
                    nc.gpsimd.indirect_dma_start(sel_rows, bass.IndirectOffsetOnAxis(slot[:, t:t + 1], 0), tok8[:, t, :], None,
                                                 bounds_check=B * KEEP - 1, oob_is_err=False).then_inc(s_sel, 16)

            def gather(bb, par):
                wait_alone(s_ids, n_of(bb, par, 1, 1))
                for kt in range(KT):
                    nc.gpsimd.indirect_dma_start(hs[:, par, kt, :], None, h_rows,
                                                 bass.IndirectOffsetOnAxis(kept_i[:, par, kt:kt + 1], 0)).then_inc(s_gh[par], 16)
                for kt in range(KT):
                    nc.gpsimd.indirect_dma_start(bs[:, par, kt, :], None, out_rows,
                                                 bass.IndirectOffsetOnAxis(kept_i[:, par, kt:kt + 1], 0)).then_inc(s_gbs[par], 16)

            store_kept(0, 0)
            gather(0, 0)

            def body(bb, par, last):
                if not last:
                    store_kept(bb + (par == 1), 1 - par)
                    gather(bb + (par == 1), 1 - par)
                pool.wait_ge(s_gb[par], bb * 16 + 16)
                for kt in range(KT):
                    pool.wait_ge(acc_out, n_of(bb, par, KT, kt + 1) + 1)
                    nc.gpsimd.tensor_tensor(y[:, par, kt, :], y[:, par, kt, :], gb_row[:, par], ALU.mult).then_inc(y_gb, 1)
                for kt in range(KT):
                    wait_alone(y_done, n_of(bb, par, KT, kt + 1) + 1)
                    nc.gpsimd.indirect_dma_start(out_rows, bass.IndirectOffsetOnAxis(kept_i[:, par, kt:kt + 1], 0), y[:, par, kt, :],
                                                 None).then_inc(s_out[par], 16)
                wait_alone(s_out[par], bb * (16 * KT) + 16 * KT)

            batches(pool, body)


def bass_adaln_block(nc, x, Wq, bq, Wk, bk, Wv, bv, temperature, w_router, W1, b1, W2, b2, c, wmod, out):
    h_rows = nc.dram_tensor("h_rows", (B * T, D), F32, kind="Internal").ap()
    mod_rows = nc.dram_tensor("mod_rows", (B, 4, D), F32, kind="Internal").ap()
    sel_rows = nc.dram_tensor("sel_rows", (B * KEEP, 2), F32, kind="Internal").ap()
    with nc.sbuf_tensor("scores", [P, 2 * NG + 2], F32) as scores:
        attention_phase(nc, x, (Wq, Wk, Wv), (bq, bk, bv), temperature, w_router, c, wmod, out, h_rows, mod_rows, scores)
        ffn_phase(nc, W1, b1, W2, b2, out, h_rows, sel_rows, mod_rows, scores)


_INS = ['L0_attn_x', 'L0_attn_Wq', 'L0_attn_bq', 'L0_attn_Wk', 'L0_attn_bk', 'L0_attn_Wv', 'L0_attn_bv', 'L0_attn_temperature',
        'L0_ffn_w_router', 'L0_ffn_W1', 'L0_ffn_b1', 'L0_ffn_W2', 'L0_ffn_b2', 'L0_c', 'L0_wmod']


def kernel(**inputs):
    import numpy as _np
    import concourse.bacc as _bacc
    from concourse import mybir as _mybir
    from concourse.bass_utils import run_bass_kernel_spmd as _run

    nc = _bacc.Bacc("TRN2", target_bir_lowering=False, num_devices=1)
    arrays, args = {}, []
    for name in _INS:
        a = _np.ascontiguousarray(inputs[name])
        arrays[f"in_{name}"] = a
        args.append(nc.dram_tensor(f"in_{name}", a.shape, _mybir.dt.from_np(a.dtype), kind="ExternalInput").ap())
    args.append(nc.dram_tensor("out_0", (B, T, D), F32, kind="ExternalOutput").ap())
    bass_adaln_block(nc, *args)
    r = _run(nc, [arrays], core_ids=[0])
    return r.results[0]["out_0"]
```

```python
from contextlib import ExitStack

import concourse.bass as bass
from concourse import mybir

P = 128
B, T, D = 8, 1024, 512
H = 16
DH = D // H
F = 2048
KEEP = T // 2
CC = D // P
FC = F // P
HG = P // DH
TG = HG * DH * 2
GB = T // TG
NG = B * GB
NQ = T // P
WS = 64.0
EPS = 1e-5
RING = 5
BIG = 1.0e6
GATE_MIN = 0.25
TB = T // P
PAD = (GB - 1) * 2 * P

ALU = mybir.AluOpType
ACT = mybir.ActivationFunctionType
AX = mybir.AxisListType
F32 = mybir.dt.float32
F16 = mybir.dt.float16
BF16 = mybir.dt.bfloat16
I32 = mybir.dt.int32


class Ranks:

    def __init__(self, nc, ctx):
        def sb(name, shape, dt=F32):
            return ctx.enter_context(nc.sbuf_tensor(name, shape, dt))

        def sem(name):
            return ctx.enter_context(nc.semaphore(name))

        self.scores = sb("scores", [P, 2 * NG + 2])
        self.srow = sb("srow", [P, T])
        self.s8 = sb("s8", [P, TB])
        self.earlier = sb("earlier", [P, 2, PAD + 2 * P + PAD], BF16)
        self.tok_i = sb("tok_i", [P, B * TB], I32)
        self.e_neg = sb("e_neg", [P, B * TB])
        self.tokens = sb("tokens", [P, B * TB, 2])
        self.tok8 = sb("tok8", [P, TB, 2])
        self.cmp_out = sb("cmp_out", [P, 2, T], BF16)
        self.above = sb("above", [P, TB])
        self.ties = sb("ties", [P, TB])
        self.rank = sb("rank", [P, TB])
        self.drop = sb("drop", [P, TB])
        self.first = sb("first", [P, 1])
        self.slot = sb("slot", [P, TB], I32)
        self.s_const = sem("s_numbers")
        self.s_srow = sem("s_srow")
        self.s_cmp = sem("s_cmp")
        self.s_rank = sem("s_rank")
        self.s_slot = sem("s_slot")
        self.s_sel = sem("s_sel")


def count_above(nc, dve, r, t, count):
    if t >= 1:
        dve.wait_ge(r.s_cmp, count(2 * TB, 2 * t - 1))
    nc.vector.tensor_scalar(r.cmp_out[:, 0], r.srow[:], r.s8[:, t:t + 1], 0.0, ALU.is_gt, ALU.add,
                            accum_out=r.above[:, t:t + 1]).then_inc(r.s_cmp, 1)
    if t >= 1:
        dve.wait_ge(r.s_cmp, count(2 * TB, 2 * t))
    at = PAD - (t // 2) * 2 * P
    nc.vector.scalar_tensor_tensor(out=r.cmp_out[:, 1], in0=r.srow[:], scalar=r.s8[:, t:t + 1],
                                   in1=r.earlier[:, t % 2, at:at + TB * P], op0=ALU.is_equal, op1=ALU.mult,
                                   accum_out=r.ties[:, t:t + 1]).then_inc(r.s_cmp, 1)


def find_slots(nc, dve, r, tokens_b, count):
    dve.wait_ge(r.s_cmp, count(2 * TB, 2 * TB))
    nc.vector.tensor_tensor(r.rank[:], r.above[:], r.ties[:], ALU.add).then_inc(r.s_rank, 1)
    dve.wait_ge(r.s_rank, count(3, 1))
    nc.vector.tensor_scalar(r.drop[:], r.rank[:], float(KEEP), BIG, ALU.is_ge, ALU.mult).then_inc(r.s_rank, 1)
    dve.wait_ge(r.s_rank, count(3, 2))
    nc.vector.tensor_copy(r.tok8[:], tokens_b)
    nc.vector.scalar_tensor_tensor(out=r.slot[:], in0=r.rank[:], scalar=r.first[:, 0:1], in1=r.drop[:],
                                   op0=ALU.add, op1=ALU.add).then_inc(r.s_slot, 1)
    nc.vector.tensor_scalar(r.first[:], r.first[:], float(KEEP), None, ALU.add).then_inc(r.s_rank, 1)
    dve.wait_ge(r.s_rank, count(3, 3))


def store_kept(nc, r, sel_rows):
    for t in range(TB):
        nc.gpsimd.indirect_dma_start(sel_rows, bass.IndirectOffsetOnAxis(r.slot[:, t:t + 1], 0), r.tok8[:, t, :], None,
                                     bounds_check=B * KEEP - 1, oob_is_err=False).then_inc(r.s_sel, 16)


def attention_phase(nc, x, w_qkv, b_qkv, temperature, w_router, c, w_mod, out, h_rows, mod_rows, sel_rows, score_rows, r):
    scores = r.scores
    Wq, Wk, Wv = w_qkv
    bq, bk, bv = b_qkv
    x_g = x.rearrange("b (g q p) d -> (b g) q p d", g=GB, p=2)
    out_g = out.rearrange("b (g q p) d -> (b g) q p d", g=GB, p=2)
    h_g = h_rows.rearrange("(n q p) d -> n q p d", n=NG, p=2)

    with ExitStack() as ctx:
        def sb(name, shape, dt):
            return ctx.enter_context(nc.sbuf_tensor(name, shape, dt))

        def pb(name, shape):
            return ctx.enter_context(nc.psum_tensor(name, shape, F32))

        def sem(name):
            return ctx.enter_context(nc.semaphore(name))

        wq16 = sb("wq16", [P, 2, CC, D], F16)
        wk16 = sb("wk16", [P, 2, CC, D], F16)
        wv16 = sb("wv16", [P, 2, CC, D], F16)
        ident = sb("ident", [P, P], F32)
        bq_col = sb("bq_col", [P, CC], F32)
        bias16 = sb("bias16", [2 * DH, 2, D], F16)
        ones16 = sb("ones16", [2 * DH, P], F16)
        router_row = sb("router_row", [P, D], F32)
        temp_col = sb("temp_col", [P, GB], F32)
        tempw_col = sb("tempw_col", [P, GB], F32)
        mod_table = sb("mod_table", [P, B + 1, 2 * CC], F32)
        mod_now = sb("mod_now", [P, 2 * CC], F32)
        rows = sb("rows", [P, 4, D], F32)
        minus_half = sb("minus_half", [P, 2], F32)
        warm = sb("warm", [P, 1], F32)
        xt = [sb(f"xt{i}", [P, 2, D], F32) for i in range(4)]
        xhat = sb("xhat", [P, 2, D], F32)
        stats1 = sb("stats1", [P, 2, 6], F32)
        mv1 = sb("mv1", [P, 2, 2], F32)
        var1 = sb("var1", [P, 2], F32)
        nmean1 = sb("nmean1", [P, 2], F32)
        rstd1 = sb("rstd1", [P, 2], F32)
        hT32 = sb("hT32", [P, CC, 2 * P], F32)
        hT16 = [sb(f"hT16_{i}", [P, 2, CC, 2 * P], F16) for i in range(2)]
        kv32 = [sb(f"kv32_{i}", [P, D], F32) for i in range(2)]
        k16 = sb("k16", [P, 2, 2 * D], F16)
        v16 = sb("v16", [P, 2, 2 * D], F16)
        stacks = [sb(f"stacks{i}", [P, 2, HG, 2 * D], F16) for i in range(2)]
        qT = [sb(f"qT{i}", [P, CC, 2 * P], F32) for i in range(2)]
        qn = sb("qn", [P, 2, HG, DH], F32)
        probs = sb("probs", [P, 2, HG, T], F32)
        nmax = sb("nmax", [P, 2, HG], F32)
        rsum = sb("rsum", [P, 2, HG], F32)
        nhalf = sb("nhalf", [P, 2], F32)
        rhalf = sb("rhalf", [P, 2], F32)
        rinv = sb("rinv", [P, 2, HG], F32)
        x2 = sb("x2", [P, 2, D], F32)
        stats2 = sb("stats2", [P, 2, 6], F32)
        mv2 = sb("mv2", [P, 2, 2], F32)
        var2 = sb("var2", [P, 2], F32)
        nmean2 = sb("nmean2", [P, 2], F32)
        rstd2 = sb("rstd2", [P, 2], F32)
        hbuf = sb("hbuf", [P, 2, 2, D], F32)
        base = sb("base", [P, 2, 2, D], F32)
        dot_out = sb("dot_out", [P, 2, D], F32)
        c_sb = sb("c_sb", [B, D], F32)
        c_e = sb("c_e", [B, D], F32)
        cT = sb("cT", [P, CC, B], F32)
        mod_b = base[0:B].rearrange("b i p d -> b (i p) d")
        mod_t = sb("mod_t", [B, 2, D], F32)
        sign, size = hbuf[0:B, 0, 0], hbuf[0:B, 0, 1]

        acc = pb("acc", [P, 2 * D])
        sc = pb("sc", [P, RING, D])
        pj = pb("pj", [P, D])

        s_c = sem("s_c")
        s_in = sem("s_in")
        s_w = [sem(f"s_w{i}") for i in range(3)]
        s_wm = [sem(f"s_wm{i}") for i in range(6)]
        s_x = [sem(f"s_x{i}") for i in range(4)]
        s_rows = sem("s_rows")
        s_modst = sem("s_modst")
        s_stk = [[sem(f"s_stk{k}{i}") for i in range(2)] for k in range(2)]
        s_st = [sem(f"s_st{i}") for i in range(2)]
        s_id = sem("s_id")
        s_idle = sem("s_idle")
        s_const = sem("s_const")
        s_v = sem("s_v")
        s_wsplit = sem("s_wsplit")
        s_ce = sem("s_ce")
        s_silu = sem("s_silu")
        s_ct = sem("s_ct")
        s_ctc = sem("s_ctc")
        s_mod = sem("s_mod")
        s_modc = sem("s_modc")
        s_modv = sem("s_modv")
        s_mt = sem("s_mt")
        s_zero = sem("s_zero")
        s_sc = sem("s_sc")
        s_exps = sem("s_exps")
        s_tok = sem("s_tok")
        s_halves = sem("s_halves")
        s_sum = sem("s_sum")
        s_bias = sem("s_bias")
        s_table = sem("s_table")
        s_now = sem("s_now")
        s_bn1 = sem("s_bn1")
        s_var1 = sem("s_var1")
        s_r1 = sem("s_r1")
        s_xhat = sem("s_xhat")
        t_pe = sem("t_pe")
        t_evac = sem("t_evac")
        s_hi = sem("s_hi")
        s_ht = sem("s_ht")
        kv_pe = sem("kv_pe")
        kv_evac = sem("kv_evac")
        kv_hi = sem("kv_hi")
        kv_split = sem("kv_split")
        q_pe = sem("q_pe")
        q_evac = sem("q_evac")
        score_pe = sem("score_pe")
        max_done = sem("max_done")
        exp_done = sem("exp_done")
        inv_done = sem("inv_done")
        qn_done = sem("qn_done")
        pv_done = sem("pv_done")
        acc_free = sem("acc_free")
        x2_done = sem("x2_done")
        s_bn2 = sem("s_bn2")
        s_agg1 = sem("s_agg1")
        s_agg2 = sem("s_agg2")
        s_dot = sem("s_dot")
        s_var2 = sem("s_var2")
        s_r2 = sem("s_r2")
        s_xh2 = sem("s_xh2")
        s_hm = sem("s_hm")
        post_done = sem("post_done")

        block = ctx.enter_context(nc.Block())

        wm_stage = [probs[:, j // 2, 2 * (j % 2):2 * (j % 2) + 2, :].rearrange("p a (b n) -> p (a b) n", n=D) for j in range(4)]
        wm_stage += [stacks[1][:, j].bitcast(F32).rearrange("p a n -> p (a n)").rearrange("p (c n) -> p c n", c=CC) for j in range(2)]
        w_stage = [stacks[0][:, j].bitcast(F32).rearrange("p a n -> p (a n)").rearrange("p (c n) -> p c n", c=CC) for j in range(2)]
        w_stage += [hbuf[:].rearrange("p a b n -> p (a b) n")]
        bias_stage = dot_out
        MOD_ORDER = (1, 0, 2, 3, 4, 5)

        UNITS = GB * NQ * HG

        firsts, at, skips = [], 0, 0
        for u in range(UNITS):
            if at == RING - 1 and u >= skips * (UNITS // GB) + 16:
                at, skips = 0, skips + 1
            firsts.append(at)
            at = (at + 2) % RING
        assert (2 * UNITS + skips) % RING == 0

        def banks(u):
            return firsts[u % UNITS], (firsts[u % UNITS] + 1) % RING

        def wraps(u):
            return banks(u)[1] == 0

        def wrapped(u):
            return sum(wraps(k) for k in range(-HG, u))

        def scores_at(u):
            a, z = banks(u)
            return sc[:, a:z + 1, :].rearrange("p a n -> p (a n)")

        def last_user(u, bank):
            return next(d for d in range(1, 6) if bank in banks(u - d))

        WRAPS = wrapped(UNITS) - wrapped(0)
        @block.sync
        def _(sp):
            for i in range(2):
                sp.sem_inc(s_st[i], 16)
            sp.dma_start(c_sb[:], c).then_inc(s_c, 16)
            sp.dma_start(xt[0][:], x_g[0]).then_inc(s_x[0], 16)

            def stage_mod(j):
                m = MOD_ORDER[j]
                sp.dma_start(wm_stage[j], w_mod[:, m * D:(m + 1) * D].rearrange("(c p) n -> p c n", p=P)).then_inc(s_wm[j], 16)

            stage_mod(0)
            stage_mod(1)
            for k, w in enumerate((Wk, Wv)):
                sp.dma_start(w_stage[k], w.rearrange("(c p) n -> p c n", p=P)).then_inc(s_w[k], 16)
            for k, b_kv in enumerate((bk, bv)):
                for row in (0, DH):
                    sp.dma_start(bias_stage[row:row + 1, k, :], b_kv.partition_broadcast(1)).then_inc(s_in, 16)
            sp.dma_start(router_row[:], w_router.partition_broadcast(P)).then_inc(s_in, 16)
            with nc.allow_non_contiguous_dma(reason="512 biases and 16 temperatures, once"):
                sp.dma_start(bq_col[:], bq.rearrange("(c p) -> p c", p=P)).then_inc(s_in, 16)
                t_hq = temperature.rearrange("(g q) a b -> q (g a b)", q=HG)
                for hq in range(HG):
                    sp.dma_start(temp_col[DH * hq:DH * (hq + 1), :], t_hq[hq].partition_broadcast(DH)).then_inc(s_in, 16)
            stage_mod(2)
            sp.dma_start(w_stage[2], Wq.rearrange("(c p) n -> p c n", p=P)).then_inc(s_w[2], 16)
            sp.dma_start(xt[1][:], x_g[1]).then_inc(s_x[1], 16)
            for j in range(3, 6):
                stage_mod(j)
            sp.dma_start(xt[2][:], x_g[2]).then_inc(s_x[2], 16)

            def replicate(m_par, k, split_count):
                src, parts = ((k16, (0, 0, 1, 1)), (v16, (0, 1, 0, 1)))[k]
                sp.wait_ge(kv_split, split_count)
                for hq in range(HG):
                    for blk in range(P // DH):
                        sp.dma_start(stacks[m_par][DH * blk:DH * (blk + 1), k, hq, :],
                                     src[DH * hq:DH * (hq + 1), parts[blk], :]).then_inc(s_stk[k][m_par], 16)

            def store_rows(n, par):
                sp.dma_start(h_g[n], hbuf[:, par]).then_inc(s_st[par], 16)
                sp.dma_start(out_g[n], base[:, par]).then_inc(s_st[par], 16)

            sp.wait_ge(s_wsplit, 6)
            replicate(0, 0, 2)
            replicate(0, 1, 4)
            sp.wait_ge(s_modv, 1)
            sp.dma_start(mod_rows, mod_b).then_inc(s_modst, 16)
            sp.wait_ge(s_modst, 16)
            with sp.Fori(0, B) as b:
                ahead = [sp.snap(b * GB + g + 3 if g + 3 < GB else ((b + 1) % B) * GB + (g + 3) % GB) for g in range(GB)]
                before = [sp.snap(b * GB + g - 1 if g >= 1 else ((b + B - 1) % B) * GB + GB - 1) for g in range(GB)]
                for g in range(GB):
                    sp.wait_ge(x2_done, b * GB + g + 1)
                    sp.dma_start(xt[(g + 3) % 4][:], x_g[ahead[g]]).then_inc(s_x[(g + 3) % 4], 16)
                    sp.wait_ge(pv_done, b * GB * NQ + g * NQ + 1)
                    sp.sem_inc(s_idle, 1)
                    replicate((g + 1) % 2, 0, b * GB * 4 + 4 * (g + 1) + 2)
                    replicate((g + 1) % 2, 1, b * GB * 4 + 4 * (g + 1) + 4)
                    sp.wait_ge(post_done, b * GB + g + 1)
                    store_rows(before[g], (g + 1) % 2)
                    if g == 0:
                        for j in range(4):
                            sp.dma_start(rows[:, j, :], mod_rows[b, j].partition_broadcast(P)).then_inc(s_rows, 16)
            def store_scores(bs):
                with nc.allow_non_contiguous_dma(reason="4 byte scores, a few thousand in all"):
                    for k in bs:
                        at = 2 + k * TB
                        sp.dma_start(score_rows[k].rearrange("(t p) -> p t", p=P), scores[:, at:at + TB]).then_inc(s_sc, 16)

            store_scores(range(B - 1))
            sp.wait_ge(s_sc, 16 * (B - 1))
            sp.dma_start(r.srow[:], score_rows[0].partition_broadcast(P)).then_inc(r.s_srow, 16)
            sp.wait_ge(s_dot, 2 * NG + 2)
            store_scores([B - 1])
            sp.wait_ge(post_done, NG + 1)
            store_rows(NG - 1, (NG - 1) % 2)
            sp.wait_ge(s_sc, 16 * B)
            for i in range(2):
                sp.wait_ge(s_st[i], 32 * (NG // 2 + i) + 16)
                for k in range(2):
                    sp.wait_ge(s_stk[k][i], 256 * (NG // 2 + 1 - i))
            for i in range(4):
                sp.wait_ge(s_x[i], 16 * (NG // 4 + (i < 3)))

        def stk_count(b, g_next):
            return b * (256 * GB // 2) + 256 * (g_next // 2 + 1)

        @block.tensor
        def _(pe):
            def scores_of(quad_g, i, hq, unit, u):
                par = quad_g % 2
                for half, bank in enumerate(banks(u)):
                    ago = last_user(u, bank)
                    if u >= 0 or unit + 2 > ago:
                        pe.wait_ge(exp_done, unit + 2 - ago)
                    mm = nc.tensor.matmul(sc[:, bank, :],
                                          stacks[par][:, 0, hq, i * P:(i + 1) * P],
                                          stacks[par][:, 1, hq, half * D:(half + 1) * D], start=True, stop=True)
                mm.then_inc(score_pe, 1)

            def kv_slice(par, kk):
                w, p = (wk16, wv16)[kk // 2], kk % 2
                nc.tensor.matmul(pj[:], ones16[:], bias16[:, kk // 2, :], start=True, stop=False)
                terms = [(cc, a, z) for cc in range(CC) for a, z in ((0, 0), (1, 0), (0, 1))]
                for t, (cc, a, z) in enumerate(terms):
                    mm = nc.tensor.matmul(pj[:], hT16[par][:, a, cc, p * P:(p + 1) * P], w[:, z, cc, :],
                                          start=False, stop=(t == len(terms) - 1))
                    if t == 5:
                        yield
                mm.then_inc(kv_pe, 1)

            def q_slice(par, s):
                for ci in range(2):
                    co = 2 * s + ci
                    terms = [(cc, a, z) for cc in range(CC) for a, z in ((0, 0), (1, 0), (0, 1))]
                    for t, (cc, a, z) in enumerate(terms):
                        mm = nc.tensor.matmul(pj[:, ci * 2 * P:(ci + 1) * 2 * P],
                                              wq16[:, z, cc, co * P:(co + 1) * P], hT16[par][:, a, cc, :],
                                              start=(t == 0), stop=(t == len(terms) - 1))
                    if ci == 0:
                        yield
                mm.then_inc(q_pe, 1)

            def t_slice(s):
                for ci in range(2):
                    for p in range(2):
                        mm = nc.tensor.transpose(pj[:, ci * 2 * P + p * P:ci * 2 * P + (p + 1) * P],
                                                 xhat[:, p, (2 * s + ci) * P:(2 * s + ci + 1) * P], ident[:])
                mm.then_inc(t_pe, 1)

            def whole(piece):
                for _ in piece:
                    pass

            def pv_half(g, i, half):
                for hq in range(HG):
                    mm = nc.tensor.matmul(acc[DH * hq:DH * (hq + 1), half * D:(half + 1) * D],
                                          qn[:, i % 2, hq, :], probs[:, i % 2, hq, half * D:(half + 1) * D],
                                          start=(i == 0), stop=(i == NQ - 1))
                if half == 1:
                    mm.then_inc(pv_done, 1)

            pe.sem_inc(pv_done, 1)
            pe.wait_ge(s_id, 2)
            pe.wait_ge(s_silu, 1)
            for cc in range(CC):
                mm = nc.tensor.transpose(pj[:, cc * B:(cc + 1) * B], c_e[:, cc * P:(cc + 1) * P], ident[0:B, 0:B])
            mm.then_inc(s_ct, 1)
            pe.wait_ge(s_ctc, 1)
            mod_banks = [sc[0:B, j, :] for j in range(4)]

            def modulate(j):
                pe.wait_ge(s_wm[j], 16)
                for cc in range(CC):
                    mm = nc.tensor.matmul(mod_banks[j % 4], cT[:, cc, :], wm_stage[j][:, cc, :], start=(cc == 0), stop=(cc == CC - 1))
                mm.then_inc(s_mod, 1)

            modulate(0)
            modulate(1)
            pe.wait_ge(s_mt, 1)
            for k in range(2 * CC):
                src = mod_t[:, k // CC, (k % CC) * P:(k % CC + 1) * P]
                mm = nc.tensor.transpose(sc[:, 4, k * B:(k + 1) * B], src, ident[0:B, 0:B])
            mm.then_inc(s_ct, 1)
            pe.wait_ge(s_xhat, 1)
            t_slice(0)
            pe.wait_ge(t_evac, 1)
            t_slice(1)
            modulate(2)
            pe.wait_ge(s_ht, 1)
            pe.wait_ge(s_bias, 3)
            for kk in range(4):
                if kk % 2 == 0:
                    pe.wait_ge(s_wsplit, 2 + kk)
                if kk >= 1:
                    pe.wait_ge(kv_evac, kk)
                whole(kv_slice(0, kk))
                if kk < 3:
                    modulate(3 + kk)
            pe.wait_ge(kv_evac, 4)
            pe.wait_ge(s_xhat, 2)
            t_slice(0)
            pe.wait_ge(t_evac, 3)
            t_slice(1)
            pe.wait_ge(t_evac, 4)
            pe.wait_ge(s_wsplit, 6)
            whole(q_slice(0, 0))
            pe.wait_ge(q_evac, 1)
            whole(q_slice(0, 1))
            for k in range(2):
                pe.wait_ge(s_stk[k][0], 256)
            pe.wait_ge(s_modc, 1)
            for hq in range(HG):
                scores_of(0, 0, hq, hq, hq - HG)

            with pe.Fori(0, B) as b:
                for g in range(GB):
                    n4 = b * (GB * 4) + 4 * (g + 1)
                    n2 = b * (GB * 2) + 2 * (g + 1)
                    for i in range(NQ):
                        nxt = (g + 1) % 2
                        piece = (kv_slice(nxt, i), kv_slice(nxt, i), kv_slice(nxt, i), kv_slice(nxt, i),
                                 None, None, q_slice(nxt, 0), q_slice(nxt, 1))[i]
                        bank_free = ((q_evac, n2), (kv_evac, n4 + 1), (kv_evac, n4 + 2), (kv_evac, n4 + 3),
                                     (kv_evac, n4 + 4), (t_evac, n2 + 3), (t_evac, n2 + 4), (q_evac, n2 + 1))[i]
                        qg, qi = (g, i + 1) if i + 1 < NQ else (g + 1, 0)
                        u = (g * NQ + i) * HG
                        unit = b * UNITS + u + HG
                        if qi == 0:
                            for k in range(2):
                                pe.wait_ge(s_stk[k][qg % 2], stk_count(b, g + 1))
                        scores_of(qg, qi, 0, unit, u)
                        if i == 0:
                            pe.wait_ge(s_ht, b * GB + g + 2)
                        if i == 4:
                            pe.wait_ge(s_xhat, b * GB + g + 3)
                        pe.wait_ge(*bank_free)
                        if piece is None:
                            t_slice(i - 4)
                        else:
                            next(piece)
                        scores_of(qg, qi, 1, unit + 1, u + 1)
                        if piece is not None:
                            whole(piece)
                        scores_of(qg, qi, 2, unit + 2, u + 2)
                        pe.wait_ge(qn_done, b * (GB * NQ) + g * NQ + i + 1)
                        if i == 0:
                            pe.wait_ge(acc_free, b * GB + g + 1)
                        pv_half(g, i, 0)
                        scores_of(qg, qi, 3, unit + 3, u + 3)
                        pv_half(g, i, 1)

        @block.scalar
        def _(act):
            act.wait_ge(s_const, 1)
            nc.scalar.activation(warm[:], warm[:], ACT.Exp).then_inc(exp_done, 1)
            act.wait_ge(s_c, 16)
            nc.scalar.activation(c_e[:], c_sb[:], ACT.Exp, scale=-1.0).then_inc(s_ce, 1)

            def evac_kv(g, kk, count, free):
                act.wait_ge(kv_pe, count)
                if free is not None:
                    act.wait_ge(kv_split, free)
                nc.scalar.activation(kv32[kk % 2][:], pj[:], ACT.Identity,
                                     scale=tempw_col[:, g:g + 1] if kk < 2 else 1.0 / WS).then_inc(kv_evac, 1)

            def evac_t(s, count):
                act.wait_ge(t_pe, count)
                for ci in range(2):
                    cc = 2 * s + ci
                    a = nc.scalar.activation(hT32[:, cc, :], pj[:, ci * 2 * P:(ci + 1) * 2 * P], ACT.Identity,
                                             bias=mod_now[:, CC + cc:CC + cc + 1], scale=mod_now[:, cc:cc + 1])
                a.then_inc(t_evac, 1)

            def evac_q(par, s, count):
                act.wait_ge(q_pe, count)
                for ci in range(2):
                    cc = 2 * s + ci
                    a = nc.scalar.activation(qT[par][:, cc, :], pj[:, ci * 2 * P:(ci + 1) * 2 * P], ACT.Identity,
                                             bias=bq_col[:, cc:cc + 1], scale=1.0 / WS)
                a.then_inc(q_evac, 1)

            def exp_unit(par, hq, count, u):
                act.wait_ge(max_done, count)
                if wraps(u):
                    for half, (bank, total) in enumerate(zip(banks(u), (rsum[:, par, hq:hq + 1], rhalf[:, par:par + 1]))):
                        a = nc.scalar.activation(probs[:, par, hq, half * D:(half + 1) * D], sc[:, bank, :], ACT.Exp,
                                                 bias=nmax[:, par, hq:hq + 1], accum_out=total)
                else:
                    a = nc.scalar.activation(probs[:, par, hq, :], scores_at(u), ACT.Exp,
                                             bias=nmax[:, par, hq:hq + 1], accum_out=rsum[:, par, hq:hq + 1])
                a.then_inc(exp_done, 1)

            act.wait_ge(s_now, 1)
            evac_t(0, 1)
            evac_t(1, 2)
            act.wait_ge(s_in, 10 * 16)
            act.wait_ge(s_bias, 1)
            for kk in range(4):
                evac_kv(0, kk, kk + 1, kk - 1 if kk >= 2 else None)
            act.wait_ge(s_ht, 1)
            evac_t(0, 3)
            evac_t(1, 4)
            evac_q(0, 0, 1)
            evac_q(0, 1, 2)
            for hq in range(HG):
                exp_unit(0, hq, hq + 1, hq - HG)
            with act.Fori(0, B) as b:
                for g in range(GB):
                    n4 = b * (GB * 4) + 4 * (g + 1)
                    n2 = b * (GB * 2) + 2 * (g + 1)
                    for i in range(NQ):
                        act.wait_ge(pv_done, b * (GB * NQ) + g * NQ + i + 1)
                        u = (g * NQ + i) * HG
                        for hq in range(HG):
                            exp_unit((i + 1) % 2, hq, b * UNITS + u + HG + hq + 1, u + hq)
                            if hq != (0 if i in (4, 5) else 1):
                                continue
                            if i < 4:
                                evac_kv((g + 1) % GB, i, n4 + i + 1, n4 + i - 1)
                            elif i < 6:
                                if i == 4 and g == 2:
                                    act.wait_ge(t_evac, n2 + 2)
                                    nc.scalar.activation(mod_now[:], mod_table[:, b + 1, :], ACT.Identity).then_inc(s_now, 1)
                                if i == 4:
                                    act.wait_ge(s_ht, b * GB + g + 2)
                                    act.wait_ge(s_now, b + 1 + (g >= 2))
                                evac_t(i - 4, n2 + i - 1)
                            else:
                                evac_q((g + 1) % 2, i - 6, n2 + i - 5)

            act.wait_ge(s_dot, 2 * NG)
            nc.scalar.activation(r.e_neg[:, 0:(B - 1) * TB], scores[:, 2:2 + (B - 1) * TB], ACT.Exp, scale=-1.0).then_inc(s_exps, 1)
            act.wait_ge(s_dot, 2 * NG + 2)
            nc.scalar.activation(r.e_neg[:, (B - 1) * TB:], scores[:, 2 + (B - 1) * TB:], ACT.Exp, scale=-1.0).then_inc(s_exps, 1)

        @block.vector
        def _(dve):
            nc.vector.memset(acc[:], 0.0)
            nc.vector.memset(warm[:], 0.0).then_inc(s_const, 1)
            nc.vector.memset(minus_half[:], -0.5).then_inc(s_const, 1)
            dve.wait_ge(s_ce, 1)
            nc.vector.tensor_scalar(mod_t[:, 0, :], c_e[:], 1.0, None, ALU.add).then_inc(s_v, 1)
            dve.wait_ge(s_v, 1)
            nc.vector.reciprocal(mod_t[:, 1, :], mod_t[:, 0, :]).then_inc(s_v, 1)
            dve.wait_ge(s_v, 2)
            nc.vector.tensor_tensor(c_e[:], c_sb[:], mod_t[:, 1, :], ALU.mult).then_inc(s_silu, 1)
            dve.wait_ge(s_ct, 1)
            nc.vector.tensor_copy(cT[:], pj[:, 0:CC * B].rearrange("p (c b) -> p c b", b=B)).then_inc(s_ctc, 1)

            def wait_alone(s, count):
                dve.wait_ge(s, count)
                dve.sem_inc(s_idle, 1)

            def stats_of_x(buf, p, loads):
                dve.wait_ge(s_x[buf], loads)
                nc.vector.bn_stats(stats1[:, p, :], xt[buf][:, p, :]).then_inc(s_bn1, 1)

            def aggregate(count):
                wait_alone(s_bn1, count * 2)
                for p in range(2):
                    st = nc.vector.bn_aggr(mv1[:, p, :], stats1[:, p, :])
                st.then_inc(s_agg1, 1)
                dve.wait_ge(s_agg1, count)
                nc.vector.tensor_scalar(var1[:], mv1[:, :, 1], EPS, None, ALU.add)
                nc.vector.tensor_scalar(nmean1[:], mv1[:, :, 0], -1.0, None, ALU.mult).then_inc(s_var1, 1)

            for p in range(2):
                stats_of_x(0, p, 16)
            aggregate(1)
            mod_banks = [sc[0:B, j, :] for j in range(4)]
            dve.wait_ge(s_mod, 1)
            nc.vector.tensor_scalar(mod_t[:, 0, :], mod_banks[0], 1.0, None, ALU.add)
            dve.wait_ge(s_mod, 2)
            nc.vector.tensor_copy(mod_t[:, 1, :], mod_banks[1]).then_inc(s_mt, 1)
            dve.wait_ge(s_ct, 2)
            tab = sc[:, 4, 0:2 * CC * B].rearrange("p (k b) -> p b k", b=B)
            nc.vector.tensor_copy(mod_table[:, B, :], tab[:, B - 1, :])
            nc.vector.tensor_copy(mod_now[:], tab[:, 0, :]).then_inc(s_now, 1)
            nc.vector.tensor_copy(mod_table[:, 0:B, :], tab).then_inc(s_table, 1)
            for k, (w16, st) in enumerate(zip((wk16, wv16, wq16), w_stage)):
                dve.wait_ge(s_w[k], 16)
                nc.vector.tensor_scalar(w16[:, 0], st, WS, None, ALU.mult).then_inc(s_wsplit, 1)
                dve.wait_ge(s_wsplit, 2 * k + 1)
                nc.vector.scalar_tensor_tensor(out=w16[:, 1], in0=st, scalar=WS, in1=w16[:, 0],
                                               op0=ALU.mult, op1=ALU.subtract).then_inc(s_wsplit, 1)
                if k == 0:
                    dve.wait_ge(s_in, 10 * 16)
                    nc.vector.tensor_scalar(tempw_col[:], temp_col[:], 1.0 / WS, None, ALU.mult).then_inc(s_bias, 1)
                    dve.wait_ge(s_bias, 2)
                    lo_row = slice(DH, DH + 1)
                    nc.vector.tensor_scalar(bias16[0:1], bias_stage[0:1], WS, None, ALU.mult)
                    nc.vector.tensor_scalar(bias16[lo_row], bias_stage[lo_row], WS, None, ALU.mult).then_inc(s_v, 1)
                    dve.wait_ge(s_v, 3)
                    nc.vector.scalar_tensor_tensor(out=bias16[lo_row], in0=bias_stage[lo_row], scalar=WS, in1=bias16[lo_row],
                                                   op0=ALU.mult, op1=ALU.subtract).then_inc(s_bias, 1)

            def row_max(par, hq, count, b, u):
                dve.wait_ge(score_pe, count)
                dst = nmax[:, par, hq:hq + 1]
                if wraps(u):
                    for half, bank in enumerate(banks(u)):
                        r = nc.vector.tensor_reduce(nhalf[:, half:half + 1], sc[:, bank, :], AX.X, ALU.max, negate=True)
                    r.then_inc(s_halves, 1)
                    dve.wait_ge(s_halves, wrapped(u) + 1 if u < 0 else b * WRAPS + (wrapped(u) + 1))
                    nc.vector.tensor_tensor(dst, nhalf[:, 0:1], nhalf[:, 1:2], ALU.min).then_inc(max_done, 1)
                else:
                    nc.vector.tensor_reduce(dst, scores_at(u), AX.X, ALU.max, negate=True).then_inc(max_done, 1)

            dve.wait_ge(s_xhat, 1)
            for p in range(2):
                stats_of_x(1, p, 16)
            aggregate(2)
            for k, (row, add) in enumerate(((0, 0.0), (2, 0.0), (1, 1.0), (3, 0.0))):
                dve.wait_ge(s_mod, k + 3)
                last = nc.vector.tensor_scalar(mod_b[:, row, :], mod_banks[(k + 2) % 4], add, None, ALU.add)
            last.then_inc(s_modc, 1)
            dve.wait_ge(s_modc, 1)
            v = 3
            for row in (0, 3):
                gate = mod_b[:, row, :]
                nc.vector.tensor_scalar(sign, gate, 0.0, 2.0, ALU.is_ge, ALU.mult).then_inc(s_v, 1)
                nc.vector.scalar_tensor_tensor(out=size, in0=gate, scalar=-1.0, in1=gate, op0=ALU.mult, op1=ALU.max).then_inc(s_v, 1)
                dve.wait_ge(s_v, v + 2)
                nc.vector.tensor_scalar(sign, sign, -1.0, None, ALU.add).then_inc(s_v, 1)
                dve.wait_ge(s_v, v + 3)
                nc.vector.scalar_tensor_tensor(out=gate, in0=size, scalar=GATE_MIN, in1=sign,
                                               op0=ALU.max, op1=ALU.mult).then_inc(s_v, 1)
                dve.wait_ge(s_v, v + 4)
                v += 4
            nc.vector.tensor_copy(size, sign).then_inc(s_modv, 1)
            for hq in range(HG):
                row_max(0, hq, hq + 1, 0, hq - HG)

            def dot_router(p, b, g):
                nc.vector.scalar_tensor_tensor(out=dot_out[:, p], in0=hbuf[:, (g + 1) % 2, p, :], scalar=1.0, in1=router_row[:],
                                               op0=ALU.mult, op1=ALU.mult,
                                               accum_out=scores[:, bass.ds(b * (2 * GB) + 2 * g + p, 1)]).then_inc(s_dot, 1)

            def gated(b, g):
                dve.wait_ge(pv_done, b * (GB * NQ) + g * NQ + 1)
                if g == 1:
                    dve.wait_ge(s_rows, b * 64 + 64)
                nc.vector.tensor_tensor(x2[:], acc[:].rearrange("q (p n) -> q p n", p=2),
                                        rows[:, 0:1, :].broadcast_to([P, 2, D]), ALU.mult).then_inc(acc_free, 1)

            def stats_of_x2(b, g, p):
                dve.wait_ge(x2_done, b * GB + g + 1)
                nc.vector.bn_stats(stats2[:, p, :], x2[:, p, :]).then_inc(s_bn2, 1)

            def aggregate2(b, g):
                wait_alone(s_bn2, b * (2 * GB) + 2 * (g + 1))
                for p in range(2):
                    st = nc.vector.bn_aggr(mv2[:, p, :], stats2[:, p, :])
                st.then_inc(s_agg2, 1)
                dve.wait_ge(s_agg2, b * GB + g + 1)
                nc.vector.tensor_scalar(var2[:], mv2[:, :, 1], EPS, None, ALU.add)
                nc.vector.tensor_scalar(nmean2[:], mv2[:, :, 0], -1.0, None, ALU.mult).then_inc(s_var2, 1)

            def whole_sum(par, hq, b, u):
                dve.wait_ge(exp_done, b * UNITS + u + HG + 2)
                total = rsum[:, par, hq:hq + 1]
                nc.vector.tensor_tensor(total, total, rhalf[:, par:par + 1], ALU.add).then_inc(s_sum, 1)

            def q_over_sums(b, g, i):
                u = (g * NQ + i) * HG
                for hq in range(2, HG):
                    if wraps(u - HG + hq):
                        whole_sum(i % 2, hq, b, u - HG + hq)
                dve.wait_ge(exp_done, b * UNITS + u + HG + 1)
                if any(wraps(u - HG + hq) for hq in range(HG)):
                    dve.wait_ge(s_sum, b * WRAPS + wrapped(u))
                nc.vector.reciprocal(rinv[:, i % 2, :], rsum[:, i % 2, :]).then_inc(inv_done, 1)
                if i == 0:
                    dve.wait_ge(q_evac, b * (2 * GB) + 2 * (g + 1))
                dve.wait_ge(inv_done, b * (GB * NQ) + g * NQ + i + 1)
                nc.vector.tensor_tensor(
                    qn[:, i % 2], qT[g % 2][:, i % CC, (i // CC) * P:(i // CC + 1) * P].rearrange("p (h j) -> p h j", j=DH),
                    rinv[:, i % 2, :].unsqueeze(2).broadcast_to([P, HG, DH]), ALU.mult).then_inc(qn_done, 1)

            for hq in range(2):
                if wraps(hq - HG):
                    whole_sum(0, hq, 0, hq - HG)
            dve.wait_ge(s_xhat, 2)
            for p in range(2):
                stats_of_x(2, p, 16)
            aggregate(3)
            with dve.Fori(0, B) as b:
                for g in range(GB):
                    for i in range(NQ):
                        par = (i + 1) % 2
                        u = (g * NQ + i) * HG
                        unit = b * UNITS + u + HG
                        for hq in range(HG):
                            row_max(par, hq, unit + hq + 1, b, u + hq)
                            if hq >= 2 and wraps(u + hq - 2):
                                whole_sum(par, hq - 2, b, u + hq - 2)
                            if hq == 0:
                                q_over_sums(b, g, i)
                            if hq == 0 and i == 0:
                                gated(b, g)
                            if hq == 1 and 1 <= i <= 2:
                                stats_of_x2(b, g, i - 1)
                            if hq == 2 and i == 2:
                                aggregate2(b, g)
                            if hq == 1 and 3 <= i <= 4:
                                if i == 3:
                                    dve.wait_ge(s_xhat, b * GB + g + 3)
                                stats_of_x((g + 3) % 4, i - 3, b * 16 + 16 * ((g + 3) // 4 + 1))
                            if hq == 2 and i == 4:
                                aggregate(b * GB + g + 4)
                            if hq == 1 and i >= 6:
                                dve.wait_ge(post_done, b * GB + g + 1)
                                dot_router(i - 6, b, g)
            gated(B, 0)
            for p in range(2):
                stats_of_x2(B, 0, p)
            aggregate2(B, 0)

            def weights(part, count):
                dve.wait_ge(s_exps, count)
                nc.vector.tensor_scalar(r.e_neg[:, part], r.e_neg[:, part], 1.0, None, ALU.add).then_inc(s_tok, 1)
                dve.wait_ge(s_tok, 2 * count)
                nc.vector.reciprocal(r.tokens[:, part, 1], r.e_neg[:, part]).then_inc(s_tok, 1)

            dve.wait_ge(r.s_const, 2)
            nc.vector.tensor_copy(r.tokens[:, :, 0], r.tok_i[:]).then_inc(s_tok, 1)
            nc.vector.memset(r.first[:], 0.0)
            nc.vector.tensor_copy(r.s8[:], scores[:, 2:2 + TB])
            weights(slice(0, (B - 1) * TB), 1)
            dve.wait_ge(s_tok, 3)
            dve.wait_ge(r.s_srow, 16)
            for t in range(TB):
                count_above(nc, dve, r, t, lambda per, off: off)
            find_slots(nc, dve, r, r.tokens[:, 0:TB, :], lambda per, off: off)
            dve.wait_ge(post_done, NG + 1)
            for p in range(2):
                dot_router(p, B, 0)
            weights(slice((B - 1) * TB, B * TB), 2)

        @block.gpsimd
        def _(pool):
            nc.gpsimd.memset(ident[:], 0.0).then_inc(s_id, 1)
            pool.wait_ge(s_id, 1)
            nc.gpsimd.affine_select(out=ident[:], in_=ident[:], compare_op=ALU.not_equal, fill=1.0, base=0,
                                    pattern=[[-1, P]], channel_multiplier=1).then_inc(s_id, 1)
            pool.wait_ge(s_const, 2)
            nc.gpsimd.memset(ones16[:], 1.0)
            nc.gpsimd.memset(bias16[:], 0.0).then_inc(s_bias, 1)
            nc.gpsimd.iota(r.tok_i[:], pattern=[[2 * P, NG], [1, 2]], base=0, channel_multiplier=2)
            for p in range(2):
                nc.gpsimd.memset(r.earlier[:, p, 0:PAD + 2 * P], 1.0)
                last = nc.gpsimd.memset(r.earlier[:, p, PAD + 2 * P:], 0.0)
            last.then_inc(r.s_const, 1)
            pool.wait_ge(r.s_const, 1)
            for p in range(2):
                for pp in range(2):
                    part = r.earlier[:, p, PAD + pp * P:PAD + (pp + 1) * P]
                    last = nc.gpsimd.affine_select(out=part, in_=part, compare_op=ALU.is_ge if p > pp else ALU.is_gt, fill=0.0,
                                                   base=0, pattern=[[-1, P]], channel_multiplier=1)
            last.then_inc(r.s_const, 1)
            nc.gpsimd.memset(rows[:], 0.0)
            nc.gpsimd.memset(xt[3][:], 0.0).then_inc(s_zero, 1)

            def wait_alone(s, count):
                pool.wait_ge(s, count)
                pool.sem_inc(s_idle, 1)

            def normed(dst, src, var, nmean, rstd, s_var, s_r, s_out, count):
                pool.wait_ge(s_var, count)
                nc.gpsimd.tensor_tensor(rstd[:], var[:], minus_half[:], ALU.pow).then_inc(s_r, 1)
                wait_alone(s_r, count)
                for p in range(2):
                    last = nc.gpsimd.tensor_scalar(dst[:, p, :], src[:, p, :], nmean[:, p:p + 1], rstd[:, p:p + 1], ALU.add, ALU.mult)
                last.then_inc(s_out, 1)

            def split_hT(par, count, t_count):
                wait_alone(t_evac, t_count)
                nc.gpsimd.tensor_scalar(hT16[par][:, 0], hT32[:], 1.0, None, ALU.mult).then_inc(s_hi, 1)
                pool.wait_ge(s_hi, count)
                nc.gpsimd.tensor_tensor(hT16[par][:, 1], hT32[:], hT16[par][:, 0], ALU.subtract).then_inc(s_ht, 1)

            def split_kv(kk, count):
                dst = (k16, v16)[kk // 2][:, :, (kk % 2) * D:(kk % 2 + 1) * D]
                wait_alone(kv_evac, count)
                nc.gpsimd.tensor_scalar(dst[:, 0], kv32[kk % 2][:], 1.0, None, ALU.mult).then_inc(kv_hi, 1)
                pool.wait_ge(kv_hi, count)
                nc.gpsimd.tensor_tensor(dst[:, 1], kv32[kk % 2][:], dst[:, 0], ALU.subtract).then_inc(kv_split, 1)

            normed(xhat, xt[0], var1, nmean1, rstd1, s_var1, s_r1, s_xhat, 1)
            split_hT(0, 1, 2)
            pool.wait_ge(t_pe, 2)
            pool.wait_ge(s_wsplit, 6)
            normed(xhat, xt[1], var1, nmean1, rstd1, s_var1, s_r1, s_xhat, 2)
            for kk in range(4):
                split_kv(kk, kk + 1)
            split_hT(1, 2, 4)

            def residual(b, g):
                pool.wait_ge(acc_free, b * GB + g + 1)
                nc.gpsimd.tensor_tensor(x2[:], x2[:], xt[(g + 3) % 4][:], ALU.add).then_inc(x2_done, 1)

            def normed_before(b, g):
                par = (g + 1) % 2
                pool.wait_ge(s_st[par], b * (32 * GB // 2) + 32 * (g // 2) + 16)
                normed(hbuf[:, par], x2, var2, nmean2, rstd2, s_var2, s_r2, s_xh2, b * GB + g + 1)

            def times_row(dst, a, row, op, done):
                nc.gpsimd.tensor_tensor(dst, a, rows[:, row:row + 1, :].broadcast_to([P, 2, D]), op).then_inc(s_hm, 1)
                pool.wait_ge(s_hm, done)

            def h_of_before(b, g):
                h = hbuf[:, (g + 1) % 2]
                pool.wait_ge(s_xh2, b * GB + g + 1)
                times_row(h, h, 1, ALU.mult, b * (3 * GB) + 3 * g + 1)
                times_row(h, h, 2, ALU.add, b * (3 * GB) + 3 * g + 2)

            def base_of_before(b, g):
                par = (g + 1) % 2
                times_row(base[:, par], hbuf[:, par], 3, ALU.mult, b * (3 * GB) + 3 * g + 3)
                nc.gpsimd.tensor_tensor(base[:, par], base[:, par], x2[:], ALU.add).then_inc(post_done, 1)

            pool.wait_ge(s_modst, 16)
            with pool.Fori(0, B) as b:
                for g in range(GB):
                    n4 = b * (GB * 4) + 4 * (g + 1)
                    n3 = b * GB + g + 3
                    residual(b, g)
                    split_kv(0, n4 + 1)
                    pool.wait_ge(t_pe, b * (2 * GB) + 2 * (g + 2))
                    normed(xhat, xt[(g + 2) % 4], var1, nmean1, rstd1, s_var1, s_r1, s_xhat, n3)
                    split_kv(1, n4 + 2)
                    normed_before(b, g)
                    split_kv(2, n4 + 3)
                    h_of_before(b, g)
                    split_kv(3, n4 + 4)
                    base_of_before(b, g)
                    split_hT(g % 2, n3, b * (2 * GB) + 2 * (g + 3))
            residual(B, 0)
            normed_before(B, 0)
            h_of_before(B, 0)
            base_of_before(B, 0)


def ffn_phase(nc, W1, b1, W2, b2, out, h_rows, sel_rows, mod_rows, score_rows, r):
    out_rows = out.rearrange("b t d -> (b t) d")
    sel_b = sel_rows.rearrange("(b k s) w -> b s k w", b=B, s=P)
    KT = KEEP // P

    with ExitStack() as ctx:
        def sb(name, shape, dt):
            return ctx.enter_context(nc.sbuf_tensor(name, shape, dt))

        def pb(name, shape):
            return ctx.enter_context(nc.psum_tensor(name, shape, F32))

        def sem(name):
            return ctx.enter_context(nc.semaphore(name))

        w1_16 = sb("w1_16", [P, 2, CC, F], F16)
        w2_16 = sb("w2_16", [P, 2, FC, D], F16)
        stage = sb("stage", [P, 4, 4, D], F32)
        b1_col = sb("b1_col", [P, FC], F32)
        b2_row = sb("b2_row", [P, D], F32)
        gb_row = sb("gb_row", [P, 2, D], F32)
        id2 = sb("id2", [P, P], F32)
        warm2 = sb("warm2", [P, 1], F32)
        kept = sb("kept", [P, 2, KT, 2], F32)
        kept_i = sb("kept_i", [P, 2, KT], I32)
        hs = sb("hs", [P, 2, KT, D], F32)
        bs = sb("bs", [P, 2, KT, D], F32)
        fT16 = sb("fT16", [P, 2, 2, CC, KEEP], F16)
        g32 = sb("g32", [P, 2, KEEP], F32)
        g16 = sb("g16", [P, 2, 2, KEEP], F16)
        y = sb("y", [P, 2, KT, D], F32)

        acc = [pb(f"ff2_{k}", [P, D]) for k in range(KT)]
        ff = [pb(f"ff1_{k}", [P, KEEP]) for k in range(2)]
        aux = [pb(f"aux{k}", [P, D]) for k in range(2)]

        s_stage = [sem(f"s_stage{i}") for i in range(8)]
        s_b = sem("s_b")
        s_gb = [sem(f"s_gb{i}") for i in range(2)]
        w_hi = sem("w_hi")
        w_lo = sem("w_lo")
        s_idle = sem("s_idle2")
        s_c2 = sem("s_c2")
        s_d = sem("s_d")
        s_s8 = sem("s_s8")
        s_kept = [sem(f"s_kept{i}") for i in range(2)]
        s_ids = sem("s_ids")
        s_gh = [sem(f"s_gh{i}") for i in range(2)]
        s_gbs = [sem(f"s_gbs{i}") for i in range(2)]
        ft_pe = sem("ft_pe")
        ft_hi = sem("ft_hi")
        ft_lo = sem("ft_lo")
        ff1_pe = sem("ff1_pe")
        gelu_done = sem("gelu_done")
        g_hi = sem("g_hi")
        g_split = sem("g_split")
        ff2_pe = sem("ff2_pe")
        acc_out = sem("acc_out")
        y_gb = sem("y_gb")
        y_w = sem("y_w")
        y_done = sem("y_done")
        s_out = [sem(f"s_out{i}") for i in range(2)]

        block = ctx.enter_context(nc.Block())

        def batches(eng, body):
            with eng.Fori(0, B // 2 - 1) as bb:
                for par in range(2):
                    body(bb, par, False, False)
            for par in range(2):
                body(B // 2 - 1, par, par == 1, True)

        def n_of(bb, par, per, off):
            return bb * (2 * per) + (per * par + off)

        @block.sync
        def _(sp):
            def load_kept(bb, par):
                with nc.allow_non_contiguous_dma(reason="number and weight of 512 tokens"):
                    sp.wait_ge(r.s_sel, n_of(bb, par, 16 * TB, 16 * TB))
                    sp.dma_start(kept[:, par], sel_b[bb * 2 + par]).then_inc(s_kept[par], 16)

            def load_scores(bat):
                sp.dma_start(r.srow[:], score_rows[bat].partition_broadcast(P)).then_inc(r.s_srow, 16)

            for j in range(8):
                if j == 5:
                    load_kept(0, 0)
                    load_scores(1)
                if j < 4:
                    src = W1[:, j * D:(j + 1) * D].rearrange("(c p) n -> p c n", p=P)
                else:
                    src = W2[(j - 4) * 4 * P:(j - 3) * 4 * P, :].rearrange("(k p) n -> p k n", p=P)
                    sp.wait_ge(w_lo, j - 3)
                sp.dma_start(stage[:, j % 4], src).then_inc(s_stage[j], 16)
                if j == 3:
                    sp.dma_start(b2_row[:], b2.partition_broadcast(P)).then_inc(s_b, 16)
                    with nc.allow_non_contiguous_dma(reason="2048 biases, once"):
                        sp.dma_start(b1_col[:], b1.rearrange("(f p) -> p f", p=P)).then_inc(s_b, 16)

            def body(bb, par, last, peeled):
                sp.wait_ge(y_done, n_of(bb, par, KT, 0) + 1)
                sp.dma_start(gb_row[:, par], mod_rows[bb * 2 + par, 3].partition_broadcast(P)).then_inc(s_gb[par], 16)
                if not last:
                    load_kept(bb + (par == 1), 1 - par)
                if not peeled:
                    load_scores(bb * 2 + par + 2)

            batches(sp, body)
            for i in range(2):
                sp.wait_ge(s_out[i], 16 * KT * B // 2)

        @block.tensor
        def _(pe):
            def transpose_kept(bb, par, cc):
                if cc == 0:
                    pe.wait_ge(s_gh[par], bb * (16 * KT) + 16 * KT)
                if cc >= 2:
                    pe.wait_ge(ft_lo, n_of(bb, par, CC, cc - 1))
                for kt in range(KT):
                    mm = nc.tensor.transpose(aux[cc % 2][:, kt * P:(kt + 1) * P], hs[:, par, kt, cc * P:(cc + 1) * P], id2[:])
                mm.then_inc(ft_pe, 1)

            def ff1(bb, par, f):
                pe.wait_ge(gelu_done, n_of(bb, par, FC, f + 1))
                if f % 4 == 0:
                    pe.wait_ge(w_lo, f // 4 + 1)
                terms = [(cc, a, z) for cc in range(CC) for z, a in ((0, 0), (0, 1), (1, 0))]
                for t, (cc, a, z) in enumerate(terms):
                    mm = nc.tensor.matmul(ff[f % 2][:], w1_16[:, z, cc, f * P:(f + 1) * P], fT16[:, par, a, cc, :],
                                          start=(t == 0), stop=(t == len(terms) - 1))
                mm.then_inc(ff1_pe, 1)

            def ff2(bb, par, f):
                if f % 4 == 0:
                    pe.wait_ge(w_lo, 4 + f // 4 + 1)
                if f == 0:
                    pe.wait_ge(acc_out, n_of(bb, par, KT, 0) + 1)
                pe.wait_ge(g_split, n_of(bb, par, FC, f + 3))
                for kt in range(KT):
                    for t, (a, z) in enumerate(((0, 0), (0, 1), (1, 0))):
                        mm = nc.tensor.matmul(acc[kt][:], g16[:, f % 2, a, kt * P:(kt + 1) * P], w2_16[:, z, f, :],
                                              start=(f == 0 and t == 0), stop=(f == FC - 1 and t == 2))
                mm.then_inc(ff2_pe, 1)

            pe.wait_ge(s_c2, 2)
            for cc in range(CC):
                transpose_kept(0, 0, cc)

            def body(bb, par, last, peeled):
                pe.wait_ge(ft_lo, n_of(bb, par, CC, CC))
                for f in range(FC):
                    ff1(bb, par, f)
                    if f >= 1:
                        ff2(bb, par, f - 1)
                    if not last and f >= FC - CC:
                        transpose_kept(bb + (par == 1), 1 - par, f - (FC - CC))
                ff2(bb, par, FC - 1)

            batches(pe, body)

        @block.scalar
        def _(act):
            def high_part(j):
                act.wait_ge(s_stage[j], 16)
                if j < 4:
                    dst = w1_16[:, 0, :, j * D:(j + 1) * D]
                else:
                    dst = w2_16[:, 0, 4 * (j - 4):4 * (j - 3), :]
                nc.scalar.activation(dst, stage[:, j % 4], ACT.Identity, scale=WS).then_inc(w_hi, 1)

            def kept_high(bb, par, cc):
                act.wait_ge(ft_pe, n_of(bb, par, CC, cc + 1))
                nc.scalar.activation(fT16[:, par, 0, cc, :], aux[cc % 2][:], ACT.Identity).then_inc(ft_hi, 1)

            act.wait_ge(s_d, 1)
            nc.scalar.activation(warm2[:], warm2[:], ACT.Gelu_apprx_tanh).then_inc(gelu_done, 2)
            for j in range(8):
                high_part(j)
            for cc in range(CC):
                kept_high(0, 0, cc)
            act.wait_ge(s_b, 32)

            def body(bb, par, last, peeled):
                for f in range(FC):
                    act.wait_ge(g_split, n_of(bb, par, FC, f + 1))
                    act.wait_ge(ff1_pe, n_of(bb, par, FC, f + 1))
                    nc.scalar.activation(g32[:, f % 2, :], ff[f % 2][:], ACT.Gelu_apprx_tanh, bias=b1_col[:, f:f + 1],
                                         scale=1.0 / WS).then_inc(gelu_done, 1)
                    if not last and f > FC - CC:
                        kept_high(bb + (par == 1), 1 - par, f - (FC - CC) - 1)
                if not last:
                    kept_high(bb + (par == 1), 1 - par, CC - 1)

            batches(act, body)

        @block.vector
        def _(dve):
            dve.sem_inc(acc_out, 1)
            dve.sem_inc(y_done, 1)
            nc.vector.memset(warm2[:], 0.0).then_inc(s_d, 1)
            nc.vector.memset(g16[:, 0, 0, 0:2], 0.0).then_inc(g_split, 2)

            def low_part(j):
                dve.wait_ge(w_hi, j + 1)
                if j < 4:
                    hi, lo = (w1_16[:, z, :, j * D:(j + 1) * D] for z in range(2))
                else:
                    hi, lo = (w2_16[:, z, 4 * (j - 4):4 * (j - 3), :] for z in range(2))
                nc.vector.scalar_tensor_tensor(out=lo, in0=stage[:, j % 4], scalar=WS, in1=hi, op0=ALU.mult,
                                               op1=ALU.subtract).then_inc(w_lo, 1)

            def numbers(bb, par):
                dve.wait_ge(s_kept[par], bb * 16 + 16)
                nc.vector.tensor_copy(kept_i[:, par], kept[:, par, :, 0]).then_inc(s_ids, 1)

            def kept_low(bb, par, cc):
                dve.wait_ge(ft_hi, n_of(bb, par, CC, cc + 1))
                nc.vector.tensor_tensor(fT16[:, par, 1, cc, :], aux[cc % 2][:], fT16[:, par, 0, cc, :], ALU.subtract).then_inc(ft_lo, 1)

            for j in range(8):
                low_part(j)
                if j == 3:
                    numbers(0, 0)
            for cc in range(CC):
                kept_low(0, 0, cc)

            def body(bb, par, last, peeled):
                nb, npar = bb + (par == 1), 1 - par
                for f in range(FC):
                    dve.wait_ge(gelu_done, n_of(bb, par, FC, f + 3))
                    nc.vector.tensor_copy(g16[:, f % 2, 0, :], g32[:, f % 2, :]).then_inc(g_hi, 1)
                    dve.wait_ge(g_hi, n_of(bb, par, FC, f + 1))
                    nc.vector.tensor_tensor(g16[:, f % 2, 1, :], g32[:, f % 2, :], g16[:, f % 2, 0, :], ALU.subtract).then_inc(g_split, 1)
                    if last:
                        continue
                    if f == 0:
                        nc.vector.tensor_copy(r.s8[:], r.scores[:, bass.ds(nb * (2 * TB) + npar * TB + 2, TB)]).then_inc(s_s8, 1)
                        dve.wait_ge(s_s8, n_of(bb, par, 1, 1))
                        dve.wait_ge(r.s_srow, n_of(nb, npar, 16, 16))
                    if f < TB:
                        count_above(nc, dve, r, f, lambda per, off: n_of(nb, npar, per, off))
                    if f == TB - 1:
                        find_slots(nc, dve, r, r.tokens[:, bass.ds(nb * (2 * TB) + npar * TB, TB), :],
                                   lambda per, off: n_of(nb, npar, per, off))
                    if f == 10:
                        numbers(nb, npar)
                    if f > FC - CC:
                        kept_low(nb, npar, f - (FC - CC) - 1)
                if not last:
                    kept_low(nb, npar, CC - 1)
                dve.wait_ge(ff2_pe, n_of(bb, par, FC, FC))
                dve.wait_ge(s_b, 32)
                for kt in range(KT):
                    nc.vector.scalar_tensor_tensor(out=y[:, par, kt, :], in0=acc[kt][:], scalar=1.0 / WS, in1=b2_row[:],
                                                   op0=ALU.mult, op1=ALU.add).then_inc(acc_out, 1)
                if not last:
                    return
                for kt in range(KT):
                    if kt == 0:
                        dve.wait_ge(s_gbs[par], bb * (16 * KT) + 16 * KT)
                    dve.wait_ge(y_gb, n_of(bb, par, KT, kt + 1))
                    nc.vector.scalar_tensor_tensor(out=y[:, par, kt, :], in0=y[:, par, kt, :], scalar=kept[:, par, kt, 1:2],
                                                   in1=bs[:, par, kt, :], op0=ALU.mult, op1=ALU.add).then_inc(y_done, 1)

            batches(dve, body)

        @block.gpsimd
        def _(pool):
            nc.gpsimd.memset(id2[:], 0.0).then_inc(s_c2, 1)
            pool.wait_ge(s_c2, 1)
            nc.gpsimd.affine_select(out=id2[:], in_=id2[:], compare_op=ALU.not_equal, fill=1.0, base=0,
                                    pattern=[[-1, P]], channel_multiplier=1).then_inc(s_c2, 1)

            def wait_alone(s, count):
                pool.wait_ge(s, count)
                pool.sem_inc(s_idle, 1)

            def gather(bb, par):
                wait_alone(s_ids, n_of(bb, par, 1, 1))
                for kt in range(KT):
                    nc.gpsimd.indirect_dma_start(hs[:, par, kt, :], None, h_rows,
                                                 bass.IndirectOffsetOnAxis(kept_i[:, par, kt:kt + 1], 0)).then_inc(s_gh[par], 16)
                for kt in range(KT):
                    nc.gpsimd.indirect_dma_start(bs[:, par, kt, :], None, out_rows,
                                                 bass.IndirectOffsetOnAxis(kept_i[:, par, kt:kt + 1], 0)).then_inc(s_gbs[par], 16)

            store_kept(nc, r, sel_rows)
            gather(0, 0)

            def body(bb, par, last, peeled):
                if not last:
                    wait_alone(r.s_slot, n_of(bb, par, 1, 2))
                    store_kept(nc, r, sel_rows)
                    gather(bb + (par == 1), 1 - par)
                pool.wait_ge(s_gb[par], bb * 16 + 16)
                for kt in range(KT):
                    yk = y[:, par, kt, :]
                    pool.wait_ge(acc_out, n_of(bb, par, KT, kt + 1) + 1)
                    nc.gpsimd.tensor_tensor(yk, yk, gb_row[:, par], ALU.mult).then_inc(y_gb, 1)
                    if last:
                        continue
                    wait_alone(y_gb, n_of(bb, par, KT, kt + 1))
                    nc.gpsimd.tensor_scalar(yk, yk, kept[:, par, kt, 1:2], None, ALU.mult).then_inc(y_w, 1)
                    if kt == 0:
                        pool.wait_ge(s_gbs[par], bb * (16 * KT) + 16 * KT)
                        pool.sem_inc(s_idle, 1)
                    pool.wait_ge(y_w, n_of(bb, par, KT, kt + 1))
                    nc.gpsimd.tensor_tensor(yk, yk, bs[:, par, kt, :], ALU.add).then_inc(y_done, 1)
                for kt in range(KT):
                    wait_alone(y_done, n_of(bb, par, KT, kt + 1) + 1)
                    nc.gpsimd.indirect_dma_start(out_rows, bass.IndirectOffsetOnAxis(kept_i[:, par, kt:kt + 1], 0), y[:, par, kt, :],
                                                 None).then_inc(s_out[par], 16)
                wait_alone(s_out[par], bb * (16 * KT) + 16 * KT)

            batches(pool, body)


def bass_adaln_block(nc, x, Wq, bq, Wk, bk, Wv, bv, temperature, w_router, W1, b1, W2, b2, c, wmod, out):
    h_rows = nc.dram_tensor("h_rows", (B * T, D), F32, kind="Internal").ap()
    mod_rows = nc.dram_tensor("mod_rows", (B, 4, D), F32, kind="Internal").ap()
    sel_rows = nc.dram_tensor("sel_rows", (B * KEEP, 2), F32, kind="Internal").ap()
    score_rows = nc.dram_tensor("score_rows", (B, T), F32, kind="Internal").ap()
    with ExitStack() as ctx:
        r = Ranks(nc, ctx)
        attention_phase(nc, x, (Wq, Wk, Wv), (bq, bk, bv), temperature, w_router, c, wmod, out, h_rows, mod_rows, sel_rows,
                        score_rows, r)
        ffn_phase(nc, W1, b1, W2, b2, out, h_rows, sel_rows, mod_rows, score_rows, r)


_INS = ['L0_attn_x', 'L0_attn_Wq', 'L0_attn_bq', 'L0_attn_Wk', 'L0_attn_bk', 'L0_attn_Wv', 'L0_attn_bv', 'L0_attn_temperature',
        'L0_ffn_w_router', 'L0_ffn_W1', 'L0_ffn_b1', 'L0_ffn_W2', 'L0_ffn_b2', 'L0_c', 'L0_wmod']


def kernel(**inputs):
    import numpy as _np
    import concourse.bacc as _bacc
    from concourse import mybir as _mybir
    from concourse.bass_utils import run_bass_kernel_spmd as _run

    nc = _bacc.Bacc("TRN2", target_bir_lowering=False, num_devices=1)
    arrays, args = {}, []
    for name in _INS:
        a = _np.ascontiguousarray(inputs[name])
        arrays[f"in_{name}"] = a
        args.append(nc.dram_tensor(f"in_{name}", a.shape, _mybir.dt.from_np(a.dtype), kind="ExternalInput").ap())
    args.append(nc.dram_tensor("out_0", (B, T, D), F32, kind="ExternalOutput").ap())
    bass_adaln_block(nc, *args)
    r = _run(nc, [arrays], core_ids=[0])
    return r.results[0]["out_0"]
```
